# Optimizing a Trainium2 kernel written in Bass

```python
import numpy as np
import jax
import jax.numpy as jnp

def _softmax(x, axis=-1):
    return jax.nn.softmax(x, axis=axis)

def _gelu(x):
    return jax.nn.gelu(x, approximate=True)

def _silu(x):
    return jax.nn.silu(x)

def _sigmoid(x):
    return jax.nn.sigmoid(x)

def _layernorm(x, axis=-1, eps=1e-05):
    m = jnp.mean(x, axis=axis, keepdims=True)
    v = jnp.var(x, axis=axis, keepdims=True)
    return (x - m) / jnp.sqrt(v + eps)

def _scatter_add(tgt, idx, src, axis=0):
    return tgt.at[idx].add(src)

def _segment_sum(src, seg, n):
    return jax.ops.segment_sum(src, seg, n)
kernel_name = 'mk_cond_resid_d4_seqx_r4_373c39'

def setup_inputs(seed: int=0):
    np.random.seed(seed)
    _w = jnp.asarray

    def _rec_inputs():
        import jax
        import jax.numpy as jnp
        _rk = jax.random.key(seed)
        x = 7.22e-05 + 1 * jax.random.normal(jax.random.fold_in(_rk, 1), (8, 256, 512), jnp.float32)
        _lenS = 256 - jax.random.randint(jax.random.fold_in(_rk, 7), (8,), 0, max(1, 256 // 4) + 1, jnp.int32)
        _lenS2 = 256 - jax.random.randint(jax.random.fold_in(_rk, 8), (8,), 0, max(1, 256 // 4) + 1, jnp.int32)
        cond_2048 = jax.random.bernoulli(jax.random.fold_in(_rk, 11), 0.8975, (8, 512)).astype(jnp.float32)
        return (x, cond_2048)
    x, cond_2048 = _rec_inputs()

    def _L0_cond_setup():
        import jax, jax.numpy as jnp
        import numpy as np
        import math
        D_MODEL = 256
        NUM_HEAD = 16
        NEG_INF = -1e+30
        key = jax.random.key(seed)
        k_x, k_m, k_q, k_k, k_v = jax.random.split(key, 5)
        B, C, T = (4, D_MODEL, 512)
        x = jax.random.normal(k_x, (B, C, T), dtype=jnp.float32)
        mask = (jax.random.uniform(k_m, (B, T)) < 0.9).astype(jnp.float32)
        limit = math.sqrt(6.0 / (C + C))
        Wq = jax.random.uniform(k_q, (C, C), minval=-limit, maxval=limit, dtype=jnp.float32)
        Wk = jax.random.uniform(k_k, (C, C), minval=-limit, maxval=limit, dtype=jnp.float32)
        Wv = jax.random.uniform(k_v, (C, C), minval=-limit, maxval=limit, dtype=jnp.float32)
        b = jnp.zeros((1,), dtype=jnp.float32)
        return {'x': x, 'mask': mask, 'Wq': Wq, 'Wk': Wk, 'Wv': Wv, 'b': b}
    _L0_cond_all = _L0_cond_setup()
    _L0_cond_in = {k: v for k, v in _L0_cond_all.items() if k in ('Wq', 'Wk', 'Wv', 'b')}
    del _L0_cond_all

    def _L1_cond_setup():
        import jax, jax.numpy as jnp
        import numpy as np
        NH = 8
        NEG = -1e+30
        key = jax.random.key(seed)
        k1, k2, k3, k4 = jax.random.split(key, 4)
        B, D, T = (4, 256, 512)
        x = jax.random.normal(k1, (B, D, T), dtype=jnp.float32)
        mask = jax.random.randint(k2, (B, T), 0, 2).astype(jnp.float32)
        lim = float(np.sqrt(6.0 / (D + D)))
        Wq = jax.random.uniform(k3, (D, D), dtype=jnp.float32, minval=-lim, maxval=lim)
        Wo = jax.random.uniform(k4, (D, D), dtype=jnp.float32, minval=-lim, maxval=lim)
        return {'x': x, 'mask': mask, 'Wq': Wq, 'Wo': Wo}
    _L1_cond_all = _L1_cond_setup()
    _L1_cond_in = {k: v for k, v in _L1_cond_all.items() if k in ('Wq', 'Wo')}
    del _L1_cond_all

    def _L2_cond_setup():
        import jax, jax.numpy as jnp
        import numpy as np
        B, T, D = (16, 128, 512)
        key = jax.random.key(seed)
        k0, k1, k2, k3 = jax.random.split(key, 4)
        scale = 1.0 / np.sqrt(D)
        return {'initial_state': jax.random.normal(k0, (B, D), jnp.float32), 'inputs': jax.random.normal(k1, (B, T, D), jnp.float32), 'W_ih': jax.random.normal(k2, (D, 3 * D), jnp.float32) * scale, 'W_hh': jax.random.normal(k3, (D, 3 * D), jnp.float32) * scale, 'b_ih': jnp.zeros((3 * D,), jnp.float32), 'b_hh': jnp.zeros((3 * D,), jnp.float32)}
    _L2_cond_all = _L2_cond_setup()
    _L2_cond_in = {k: v for k, v in _L2_cond_all.items() if k in ('W_ih', 'W_hh', 'b_ih', 'b_hh')}
    del _L2_cond_all

    def _L3_cond_setup():
        import jax, jax.numpy as jnp
        import numpy as np
        NUM_BLOCKS = 8
        NUM_LAYERS = 4
        EPS = 1e-06
        key = jax.random.key(seed)
        ks = jax.random.split(key, 6)
        B, S, H = (4, 1024, 512)
        inputs = jax.random.normal(ks[0], (B, S, H), dtype=jnp.float32)
        query_vectors = jax.random.normal(ks[1], (NUM_LAYERS, H), dtype=jnp.float32) * 0.01
        lim = float(np.sqrt(6.0 / (H + H)))
        Wk = jax.random.uniform(ks[2], (H, H), minval=-lim, maxval=lim, dtype=jnp.float32)
        Wo = jax.random.uniform(ks[3], (H, H), minval=-lim, maxval=lim, dtype=jnp.float32)
        rms_weight = jnp.ones((H,), dtype=jnp.float32)
        ln_gamma = jnp.ones((H,), dtype=jnp.float32)
        ln_beta = jnp.zeros((H,), dtype=jnp.float32)
        return {'inputs': inputs, 'layer_idx': 1, 'rms_weight': rms_weight, 'query_vectors': query_vectors, 'Wk': Wk, 'Wo': Wo, 'ln_gamma': ln_gamma, 'ln_beta': ln_beta}
    _L3_cond_all = _L3_cond_setup()
    _L3_cond_in = {k: v for k, v in _L3_cond_all.items() if k in ('rms_weight', 'Wk', 'Wo', 'ln_gamma', 'ln_beta')}
    del _L3_cond_all
    return {'x': x, 'cond_2048': cond_2048, 'L0_cond_Wq': _L0_cond_in['Wq'], 'L0_cond_Wk': _L0_cond_in['Wk'], 'L0_cond_Wv': _L0_cond_in['Wv'], 'L0_cond_b': _L0_cond_in['b'], 'L1_cond_Wq': _L1_cond_in['Wq'], 'L1_cond_Wo': _L1_cond_in['Wo'], 'L2_cond_W_ih': _L2_cond_in['W_ih'], 'L2_cond_W_hh': _L2_cond_in['W_hh'], 'L2_cond_b_ih': _L2_cond_in['b_ih'], 'L2_cond_b_hh': _L2_cond_in['b_hh'], 'L3_cond_rms_weight': _L3_cond_in['rms_weight'], 'L3_cond_Wk': _L3_cond_in['Wk'], 'L3_cond_Wo': _L3_cond_in['Wo'], 'L3_cond_ln_gamma': _L3_cond_in['ln_gamma'], 'L3_cond_ln_beta': _L3_cond_in['ln_beta']}

def reference(x, cond_2048, L0_cond_Wq, L0_cond_Wk, L0_cond_Wv, L0_cond_b, L1_cond_Wq, L1_cond_Wo, L2_cond_W_ih, L2_cond_W_hh, L2_cond_b_ih, L2_cond_b_hh, L3_cond_rms_weight, L3_cond_Wk, L3_cond_Wo, L3_cond_ln_gamma, L3_cond_ln_beta):
    import jax
    import jax.numpy as jnp

    def _L0_cond_ref(x, mask, Wq, Wk, Wv, b):
        import jax, jax.numpy as jnp
        import numpy as np
        import math
        D_MODEL = 256
        NUM_HEAD = 16
        NEG_INF = -1e+30
        B, C, T = x.shape
        H = NUM_HEAD
        Dh = C // H

        def proj(W):
            y = jnp.einsum('oc,bct->bto', W, x)
            return y.reshape(B, T, H, Dh).transpose(0, 2, 1, 3)
        Q, K, V = (proj(Wq), proj(Wk), proj(Wv))
        att = jnp.einsum('bhqd,bhkd->bhqk', Q, K) * (1.0 / math.sqrt(Dh))
        att = att + b[0]
        m = mask[:, None, None, :]
        att = att * m + (1.0 - m) * NEG_INF
        att = jax.nn.softmax(att, axis=-1)
        y = jnp.einsum('bhqk,bhkd->bhqd', att, V)
        y = y.transpose(0, 2, 1, 3).reshape(B, T, C)
        return y.transpose(0, 2, 1)

    def _L1_cond_ref(x, mask, Wq, Wo):
        import jax, jax.numpy as jnp
        import numpy as np
        NH = 8
        NEG = -1e+30
        B, D, T = x.shape
        dk = D // NH
        scale = 1.0 / jnp.sqrt(jnp.asarray(dk, x.dtype))
        xt = jnp.transpose(x, (0, 2, 1))
        q = xt @ Wq.T
        qh = q.reshape(B, T, NH, dk).transpose(0, 2, 1, 3)
        scores = scale * jnp.einsum('bhqd,bhkd->bhqk', qh, qh)
        cmask = mask[:, None, None, :]
        rmask = mask[:, None, :, None]
        logits = (scores * cmask + (1.0 - cmask) * NEG) * rmask
        attn = jax.nn.softmax(logits, axis=-1)
        ctx = jnp.einsum('bhqk,bhkd->bhqd', attn, qh)
        ctx = ctx.transpose(0, 2, 1, 3).reshape(B, T, D)
        out = ctx @ Wo.T
        return jnp.transpose(out, (0, 2, 1))

    def _L2_cond_ref(initial_state, inputs, W_ih, W_hh, b_ih, b_hh):
        import jax, jax.numpy as jnp
        import numpy as np
        B, T, D = (16, 128, 512)
        "ScanOverTime(GRU cell): sequential per-timestep module call with\n            dict-state passing; merge_dict_trees stacks the per-step\n            'state_predicted' tensors along axis=1 -> [B, T, D]."

        def cell(h, x):
            gi = x @ W_ih + b_ih
            gh = h @ W_hh + b_hh
            i_r, i_z, i_n = jnp.split(gi, 3, axis=-1)
            h_r, h_z, h_n = jnp.split(gh, 3, axis=-1)
            r = jax.nn.sigmoid(i_r + h_r)
            z = jax.nn.sigmoid(i_z + h_z)
            n = jnp.tanh(i_n + r * h_n)
            h_new = (1.0 - z) * n + z * h
            return (h_new, h_new)
        xs = jnp.swapaxes(inputs, 0, 1)
        _, hs = jax.lax.scan(cell, initial_state, xs)
        return jnp.swapaxes(hs, 0, 1)

    def _L3_cond_ref(inputs, layer_idx, rms_weight, query_vectors, Wk, Wo, ln_gamma, ln_beta):
        import jax, jax.numpy as jnp
        import numpy as np
        NUM_BLOCKS = 8
        NUM_LAYERS = 4
        EPS = 1e-06
        B, S, H = inputs.shape
        block_size = max(1, S // NUM_BLOCKS)
        n_blocks = S // block_size
        block_repr = inputs.reshape(B, n_blocks, block_size, H).sum(axis=2)
        keys = jnp.einsum('bnh,kh->bnk', block_repr, Wk)
        rms = jnp.sqrt(jnp.mean(keys * keys, axis=-1, keepdims=True) + EPS)
        keys = keys / rms * rms_weight
        q = query_vectors[layer_idx]
        scores = jnp.einsum('bnh,h->bn', keys, q)
        attn = jax.nn.softmax(scores, axis=-1)
        attended = jnp.einsum('bn,bnh->bh', attn, block_repr)
        attended = jnp.broadcast_to(attended[:, None, :], (B, S, H))
        proj = jnp.einsum('bsh,kh->bsk', attended, Wo)
        x = inputs + proj
        mu = jnp.mean(x, axis=-1, keepdims=True)
        var = jnp.mean((x - mu) ** 2, axis=-1, keepdims=True)
        out = (x - mu) / jnp.sqrt(var + EPS) * ln_gamma + ln_beta
        return out
    x = x + _L0_cond_ref(x, cond_2048, L0_cond_Wq, L0_cond_Wk, L0_cond_Wv, L0_cond_b)
    x = x + _L1_cond_ref(x, cond_2048, L1_cond_Wq, L1_cond_Wo)
    x = x + _L2_cond_ref(cond_2048, x, L2_cond_W_ih, L2_cond_W_hh, L2_cond_b_ih, L2_cond_b_hh)
    x = x + _L3_cond_ref(x, 1, L3_cond_rms_weight, cond_2048, L3_cond_Wk, L3_cond_Wo, L3_cond_ln_gamma, L3_cond_ln_beta)
    return x

_drawn_inputs = setup_inputs


def setup_inputs(seed=0):
    import zlib

    import numpy as np

    out = dict(_drawn_inputs(seed))
    spreads = {'L2_cond_b_ih': (0.0, 0.1),
     'L2_cond_b_hh': (0.0, 0.1),
     'L3_cond_rms_weight': (1.0, 0.2),
     'L3_cond_ln_gamma': (1.0, 0.2),
     'L3_cond_ln_beta': (0.0, 0.1)}
    factors = {}
    for name, (base, spread) in spreads.items():
        noise = np.random.default_rng([zlib.crc32(name.encode()), seed]).standard_normal(out[name].shape)
        drawn = base * np.exp(spread * noise) if base else spread * noise
        out[name] = jnp.asarray(drawn.astype(out[name].dtype))
    for name, factor in factors.items():
        out[name] = (out[name] * factor).astype(out[name].dtype)
    return out
```

```python
import concourse.bass as bass
from concourse import mybir
from contextlib import ExitStack


def attention_layers(nc, xT, x, mask, wq0, wk0, wv0, b0, wq1, wo1, ident_in):
    fp32 = mybir.dt.float32
    bf16 = mybir.dt.bfloat16
    ALU = mybir.AluOpType
    ACT = mybir.ActivationFunctionType
    AX = mybir.AxisListType
    P = 128
    B = x.shape[2]
    T = x.shape[3]
    CH = 2 * P
    KC = T // P
    NEG = 1e30
    HEADS = (16, 8)
    DH = (16, 32)
    SCALE = (1.0 / 4.0, float(1.0 / 32.0 ** 0.5))
    UNITS = [(0, g) for g in range(4)] + [(1, g) for g in range(2)]
    NU = len(UNITS)
    with ExitStack() as ctx:
        def sb(name, shape, dt=fp32):
            return ctx.enter_context(nc.sbuf_tensor(name, shape, dt))
        def pb(name, shape, dt=fp32):
            return ctx.enter_context(nc.psum_tensor(name, shape, dt))
        def sem(name):
            return ctx.enter_context(nc.semaphore(name))
        xc = sb("xc", [P, 2, T])
        w0 = sb("w0", [P, 3, 2, CH])
        w1 = sb("w1", [P, 2, 2, CH])
        ident = sb("ident", [P, P])
        ones = sb("ones", [P, 32])
        sel = sb("sel", [P, 4])
        qk = sb("qk", [P, 2, 2, T])
        qp = sb("qp", [P, 4, T])
        kp = sb("kp", [P, 4, T])
        va = sb("va", [P, KC, 16, 32])
        vb = sb("vb", [P, KC, CH])
        q1 = sb("q1", [P, 2, T])
        q1m = sb("q1m", [P, 2, T])
        mbc = sb("mbc", [P, T])
        anyc = sb("anyc", [P, 1])
        augk = sb("augk", [P, T], bf16)
        augq = sb("augq", [P, 2, T], bf16)
        mx = sb("mx", [P, 2, 16])
        nm = sb("nm", [16, 2, P])
        nhi = sb("nhi", [16, P], bf16)
        nlo = sb("nlo", [16, P], bf16)
        pr = sb("pr", [P, 2, 4, T])
        raw = sb("raw", [P, T])
        rawd = sb("rawd", [P, T])
        raw2 = sb("raw2", [P, 2, T])
        rd = sb("rd", [P, 16])
        yT = sb("yT", [P, KC, CH])
        m8 = sb("m8", [B, T]); any8 = sb("any8", [B, 1]); b8 = sb("b8", [B, 1]); mb8 = sb("mb8", [B, T])
        mb8h = sb("mb8h", [B, T], bf16); m8h = sb("m8h", [B, T], bf16)
        d_any = nc.dram_tensor("d_any", [B, 1], fp32, kind="Internal").ap()
        d_mb = nc.dram_tensor("d_mb", [B, T], fp32, kind="Internal").ap()
        d_mbh = nc.dram_tensor("d_mbh", [B, T], bf16, kind="Internal").ap()
        d_mh = nc.dram_tensor("d_mh", [B, T], bf16, kind="Internal").ap()
        MX = [pb(f"MX{i}", [P, T]) for i in range(2)]
        ST = pb("ST", [P, 4 * T])
        AV = pb("AV", [P, T])
        DN = pb("DN", [P, T])
        def bank(i):
            return ST[:, i * T:(i + 1) * T]

        class Signal:
            def __init__(self, name, per, prime=0):
                self.sem, self.per, self.prime = sem(name), per, prime

            def at(self, b, n):
                return b * self.per + (n + self.prime)

        weights, const, masks_in, masks_out, scratch, written = (sem(n) for n in (
            "weights", "const", "masks_in", "masks_out", "scratch", "written"))
        xload = Signal("xload", 16)
        mload = Signal("mload", 16 * 9)
        proj_mm = Signal("proj_mm", 6)
        q_ev = Signal("q_ev", 2)
        k_ev = Signal("k_ev", 2)
        q1_ev = Signal("q1_ev", 2)
        q_mask = Signal("q_mask", 2)
        v_mm = Signal("v_mm", 4)
        v_ev = Signal("v_ev", 4)
        spread = Signal("spread", 16 * 32)
        mx_mm = Signal("mx_mm", 16 * NU)
        mx_red = Signal("mx_red", 16 * NU, 2)
        mxT_mm = Signal("mxT_mm", NU, 2)
        nm_row = Signal("nm_row", NU)
        nsplit = Signal("nsplit", 4)
        nm_dma = Signal("nm_dma", 32 * NU, 64)
        st_mm = Signal("st_mm", 8 * NU)
        exped = Signal("exped", 8 * NU, 2)
        av_mm = Signal("av_mm", 4 * NU, 2)
        raw_ev = Signal("raw_ev", NU, 1)
        rawd_ev = Signal("rawd_ev", 2, 1)
        fin_mm = Signal("fin_mm", NU, 1)
        rden = Signal("rden", NU)
        yn = Signal("yn", NU, 1)
        back_mm = Signal("back_mm", 4, 4)
        x1 = Signal("x1", 2)
        ctx_ev = Signal("ctx_ev", 2)
        lo_mm = Signal("lo_mm", 4, 4)
        xT_ev = Signal("xT_ev", 4, 4)
        PRIMED = (mx_red, mxT_mm, nm_dma, exped, av_mm, raw_ev, rawd_ev, fin_mm, yn, back_mm, lo_mm, xT_ev)
        block = ctx.enter_context(nc.Block())

        def wait(eng, signal, b, n):
            eng.wait_ge(signal.sem, signal.at(b, n))

        def units(L):
            return [w for w in range(NU) if UNITS[w][0] == L]

        @block.sync
        def _(sp):
            sp.dma_start(m8[:], mask).then_inc(masks_in, 16)
            sp.dma_start(b8[:], b0.rearrange("(a n) -> a n", a=1).to_broadcast([B, 1])).then_inc(masks_in, 16)
            for i, d in enumerate((wq0, wk0, wv0)):
                sp.dma_start(w0[:, i], d).then_inc(weights, 16)
            for i, d in enumerate((wq1, wo1)):
                sp.dma_start(w1[:, i], d).then_inc(weights, 16)
            sp.dma_start(ident[:], ident_in).then_inc(weights, 16)
            sp.wait_ge(masks_out, 6)
            sp.dma_start(d_any, any8[:]).then_inc(scratch, 16)
            sp.dma_start(d_mb, mb8[:]).then_inc(scratch, 16)
            sp.dma_start(d_mbh, mb8h[:]).then_inc(scratch, 16)
            sp.dma_start(d_mh, m8h[:]).then_inc(scratch, 16)
            sp.wait_ge(scratch, 64)
            sp.wait_ge(const, 8)
            with sp.Fori(0, B) as b:
                wait(sp, lo_mm, b, 0)
                sp.dma_start(xc[:], x[:, :, bass.ds(b, 1), :].rearrange("p k b t -> p k (b t)")).then_inc(xload.sem, 16)
                row = bass.ds(b, 1)
                sp.dma_start(mbc[:], mask[row, :].to_broadcast([P, T])).then_inc(mload.sem, 16)
                sp.dma_start(anyc[:], d_any[row, :].to_broadcast([P, 1])).then_inc(mload.sem, 16)
                for g in range(4):
                    sp.dma_start(kp[16:16 + 97:32, g, :], d_mb[row, :].to_broadcast([4, T])).then_inc(mload.sem, 16)
                sp.dma_start(augk[0:97:32, :], d_mbh[row, :].to_broadcast([4, T])).then_inc(mload.sem, 16)
                for g in range(2):
                    sp.dma_start(augq[0:97:32, g, :], d_mh[row, :].to_broadcast([4, T])).then_inc(mload.sem, 16)
                for m in range(2):
                    for i, (dst, ready) in enumerate(((qp, q_ev), (kp, k_ev))):
                        wait(sp, ready, b, m + 1)
                        for h in range(8):
                            sp.dma_start(dst[32 * (h % 4):32 * (h % 4) + 16, 2 * m + h // 4, :],
                                         qk[16 * h:16 * h + 16, i, m, :]).then_inc(spread.sem, 16)
                for w, (L, g) in enumerate(UNITS):
                    if L == 0:
                        wait(sp, nm_row, b, w + 1)
                        sp.dma_start(qp[17:17 + 97:32, g, :], nm[:, w % 2, :]).then_inc(nm_dma.sem, 32)
                    else:
                        wait(sp, nsplit, b, 2 * g + 2)
                        sp.dma_start(augq[1:98:32, g, :], nhi[:]).then_inc(nm_dma.sem, 16)
                        sp.dma_start(augq[2:99:32, g, :], nlo[:]).then_inc(nm_dma.sem, 16)
            wait(sp, xT_ev, B - 1, 4)

        @block.gpsimd
        def _(pool):
            for buf in (ones, qp, kp, va, augk, augq):
                pool.memset(buf[:], 1.0).then_inc(const, 1)
            pool.wait_ge(weights, 96)
            pool.tensor_copy(sel[:], ident[:, 0:97:32]).then_inc(const, 1)
            for s in PRIMED:
                pool.sem_inc(s.sem, s.prime)

        @block.vector
        def _(dve):
            dve.memset(AV[:], 0.0).then_inc(const, 1)
            dve.wait_ge(masks_in, 32)
            dve.reduce_max(any8[:], m8[:], AX.X).then_inc(masks_out, 1)
            dve.tensor_scalar(mb8[:], m8[:], NEG, -NEG, ALU.mult, ALU.add).then_inc(masks_out, 1)
            dve.wait_ge(masks_out, 2)
            dve.tensor_copy(mb8h[:], mb8[:]).then_inc(masks_out, 1)
            dve.tensor_copy(m8h[:], m8[:]).then_inc(masks_out, 1)
            dve.tensor_scalar(b8[:], b8[:], 1.0 / SCALE[0], None, ALU.mult).then_inc(masks_out, 1)
            dve.wait_ge(masks_out, 5)
            dve.tensor_scalar(mb8[:], mb8[:], b8[:, 0:1], any8[:, 0:1], ALU.add, ALU.mult).then_inc(masks_out, 1)

            def reduces(b, w):
                wait(dve, mxT_mm, b, w - 1)
                for n in range(16):
                    qb, i = divmod(n, 4)
                    wait(dve, mx_mm, b, 16 * w + n + 1)
                    dve.reduce_max(mx[:, w % 2, 4 * i + qb:4 * i + qb + 1], MX[n % 2][:, :], AX.X).then_inc(mx_red.sem, 1)

            def normalise(b, w):
                L, g = UNITS[w]
                dh = DH[L]
                wait(dve, fin_mm, b, w + 1)
                y = DN[:, :].rearrange("p (q i d) -> p q i d", q=KC, i=4)
                den = y[:, :, :, 16] if L == 0 else AV[:, 0:16].rearrange("p (q i) -> p q i", q=KC)
                dve.reciprocal(rd[:].rearrange("p (q i) -> p q i", q=KC), den).then_inc(rden.sem, 1)
                wait(dve, rden, b, w + 1)
                if g == 0:
                    wait(dve, back_mm, b, 2 * L)
                for qb in range(KC):
                    last = dve.tensor_tensor(
                        yT[:, qb, 4 * dh * g:4 * dh * (g + 1)].rearrange("p (i d) -> p i d", i=4), y[:, qb, :, 0:dh],
                        rd[:, 4 * qb:4 * qb + 4].rearrange("p (i a) -> p i a", a=1).to_broadcast([P, 4, dh]), ALU.mult)
                last.then_inc(yn.sem, 1)

            def split_max(b, w):
                g = UNITS[w][1]
                wait(dve, nm_row, b, w + 1)
                wait(dve, nm_dma, b, 32 * (w - 1 if g else w - 5))
                if g:
                    wait(dve, nm_dma, b, 32 * w)
                dve.tensor_copy(nhi[:], nm[:, w % 2, :]).then_inc(nsplit.sem, 1)
                wait(dve, nsplit, b, 2 * g + 1)
                dve.tensor_tensor(nlo[:], nm[:, w % 2, :], nhi[:], ALU.subtract).then_inc(nsplit.sem, 1)

            dve.wait_ge(const, 8)
            with dve.Fori(0, B) as b:
                for m in range(2):
                    wait(dve, proj_mm, b, 2 * m + 2)
                    if m == 0:
                        wait(dve, spread, b, 0) if False else None
                    dve.tensor_copy(qk[:, 1, m, :], bank(2 * m + 1)).then_inc(k_ev.sem, 1)
                for m in range(2):
                    wait(dve, v_mm, b, m + 1)
                    dve.tensor_copy(va[:, 2 * m:2 * m + 2, :, 0:16],
                                    MX[m][:, :].rearrange("p (k h d) -> p k h d", k=2, h=16)).then_inc(v_ev.sem, 1)
                for L in range(2):
                    ws = units(L)
                    if L == 1:
                        for m in range(2):
                            wait(dve, v_mm, b, m + 3)
                            dve.tensor_copy(vb[:, 2 * m:2 * m + 2, :], MX[m][:, :].rearrange("p (k h) -> p k h", k=2)).then_inc(v_ev.sem, 1)
                        for m in range(2):
                            wait(dve, q1_ev, b, m + 1)
                            dve.tensor_tensor(q1m[:, m, :], q1[:, m, :], mbc[:], ALU.mult).then_inc(q_mask.sem, 1)
                    reduces(b, ws[0])
                    if L == 1:
                        split_max(b, ws[0])
                    for w in ws:
                        if w > ws[0]:
                            normalise(b, w - 1)
                        if w + 1 in ws:
                            reduces(b, w + 1)
                            if L == 1:
                                split_max(b, w + 1)
                    normalise(b, ws[-1])
                    if L == 0:
                        for m in range(2):
                            wait(dve, back_mm, b, m + 1)
                            dve.tensor_tensor(xc[:, m, :], xc[:, m, :], bank(m), ALU.add).then_inc(x1.sem, 1)

        @block.scalar
        def _(act):
            def maxrow(b, w):
                wait(act, mxT_mm, b, w + 1)
                wait(act, nm_dma, b, 32 * (w - 1))
                if UNITS[w][0] == 1:
                    pass
                act.activation(nm[:, w % 2, :], MX[0][0:16, 0:P], ACT.Copy, scale=-1.0).then_inc(nm_row.sem, 1)

            def raw_copy(b, w):
                wait(act, av_mm, b, 4 * w + 4)
                wait(act, fin_mm, b, w)
                act.copy(raw[:], AV[:, :]).then_inc(raw_ev.sem, 1)
                if UNITS[w][0] == 1:
                    act.copy(rawd[:], DN[:, :]).then_inc(rawd_ev.sem, 1)

            with act.Fori(0, B) as b:
                wait(act, mload, b, 144)
                for L in range(2):
                    ws = units(L)
                    for m in range(2):
                        if L == 0:
                            wait(act, proj_mm, b, 2 * m + 1)
                            act.activation(qk[:, 0, m, :], bank(2 * m), ACT.Copy, scale=anyc[:, 0:1]).then_inc(q_ev.sem, 1)
                        else:
                            wait(act, proj_mm, b, 5 + m)
                            act.copy(q1[:, m, :], bank(m)).then_inc(q1_ev.sem, 1)
                    maxrow(b, ws[0])
                    for w in ws:
                        for kc in range(KC):
                            wait(act, av_mm, b, 4 * w + kc - 1)
                            for p in range(2):
                                wait(act, st_mm, b, 8 * w + 2 * kc + p + 1)
                                act.activation(pr[:, kc % 2, 2 * p:2 * p + 2, :],
                                               ST[:, 2 * p * T:(2 * p + 2) * T].rearrange("p (a t) -> p a t", a=2),
                                               ACT.Exp, scale=SCALE[L]).then_inc(exped.sem, 1)
                            if kc == 0 and w > ws[0]:
                                raw_copy(b, w - 1)
                            if kc == 2 and w + 1 in ws:
                                maxrow(b, w + 1)
                    raw_copy(b, ws[-1])
                    if L == 1:
                        for m in range(2):
                            wait(act, back_mm, b, 3 + m)
                            act.copy(raw2[:, m, :], bank(m)).then_inc(ctx_ev.sem, 1)
                        for c in range(KC):
                            wait(act, lo_mm, b, c + 1)
                            act.copy(xT[:, c, :, bass.ds(b, 1)].rearrange("p o b -> p (o b)"), bank(2 + c % 2)[:, 0:CH]).then_inc(xT_ev.sem, 1)

        @block.tensor
        def _(pe):
            def max_pass(b, w, qbs, heads=(0, 1, 2, 3)):
                L, g = UNITS[w]
                for qb in qbs:
                    for i in heads:
                        n = 4 * qb + i
                        wait(pe, mx_red, b, 16 * w + n - 1)
                        o = MX[n % 2][:, :]
                        q0 = slice(qb * P, (qb + 1) * P)
                        if L == 0:
                            r = slice(32 * i, 32 * i + 17)
                            pe.matmul(o, qp[r, g, q0], kp[r, g, :], start=True, stop=True).then_inc(mx_mm.sem, 1)
                        else:
                            r = slice(32 * i, 32 * i + 32)
                            a = slice(32 * i, 32 * i + 1)
                            pe.matmul(o, q1m[r, g, q0], q1[r, g, :], start=True, stop=False)
                            pe.matmul(o, augq[a, g, q0], augk[a, :], start=False, stop=True).then_inc(mx_mm.sem, 1)

            def max_transpose(b, w):
                wait(pe, mx_red, b, 16 * w + 16)
                pe.matmul(MX[0][0:16, 0:P], mx[:, w % 2, :], ident[:], start=True, stop=True).then_inc(mxT_mm.sem, 1)

            def scores(b, w, kc):
                L, g = UNITS[w]
                k0 = slice(kc * P, (kc + 1) * P)
                for i in range(4):
                    if i % 2 == 0:
                        wait(pe, exped, b, 8 * w + 2 * kc + i // 2 - 1)
                    if L == 0:
                        r = slice(32 * i, 32 * i + 18)
                        last = pe.matmul(bank(i), kp[r, g, k0], qp[r, g, :], start=True, stop=True)
                    else:
                        r = slice(32 * i, 32 * i + 32)
                        a = slice(32 * i, 32 * i + 3)
                        pe.matmul(bank(i), q1[r, g, k0], q1m[r, g, :], start=True, stop=False)
                        last = pe.matmul(bank(i), augk[a, k0], augq[a, g, :], start=False, stop=True)
                    if i % 2 == 1:
                        last.then_inc(st_mm.sem, 1)

            def values(b, w, kc):
                L, g = UNITS[w]
                if kc == 0:
                    wait(pe, raw_ev, b, w)
                    if L == 1:
                        wait(pe, yn, b, w)
                        wait(pe, rawd_ev, b, g)
                wait(pe, exped, b, 8 * w + 2 * kc + 2)
                for i in range(4):
                    r = slice(32 * i, 32 * i + (17 if L == 0 else 32))
                    v = va[:, kc, 4 * g + i, 0:17] if L == 0 else vb[:, kc, 128 * g + 32 * i:128 * g + 32 * i + 32]
                    last = pe.matmul(AV[r, :], v, pr[:, kc % 2, i, :], start=kc == 0, stop=kc == KC - 1)
                if L == 1:
                    for i in range(4):
                        r = slice(32 * i, 32 * i + 32)
                        last = pe.matmul(DN[r, :], ones[:, :], pr[:, kc % 2, i, :], start=kc == 0, stop=kc == KC - 1)
                last.then_inc(av_mm.sem, 1)

            def finish(b, w):
                L, g = UNITS[w]
                wait(pe, raw_ev, b, w + 1)
                wait(pe, yn, b, w)
                if L == 1:
                    wait(pe, rawd_ev, b, g + 1)
                    for qb in range(KC):
                        pe.matmul(AV[:, 4 * qb:4 * qb + 4], rawd[:, qb * P:(qb + 1) * P], sel[:], start=qb == 0, stop=qb == KC - 1, skip_group_check=True)
                for qb in range(KC):
                    last = pe.transpose(DN[:, qb * P:(qb + 1) * P], raw[:, qb * P:(qb + 1) * P], ident[:])
                last.then_inc(fin_mm.sem, 1)

            def project(b, o, w_, m, src):
                for k in range(2):
                    last = pe.matmul(o, w_[:, k, m * P:(m + 1) * P], src[:, k, :], start=k == 0, stop=k == 1)
                last.then_inc(proj_mm.sem, 1)

            def project_rows(b, w_, src):
                for m in range(2):
                    for h in range(2):
                        c = 2 * m + h
                        for k in range(2):
                            last = pe.matmul(MX[m][:, h * CH:(h + 1) * CH], src[:, k, c * P:(c + 1) * P], w_[:, k, :],
                                             start=k == 0, stop=k == 1)
                    last.then_inc(v_mm.sem, 1)

            pe.wait_ge(weights, 96)
            pe.wait_ge(const, 8)
            with pe.Fori(0, B) as b:
                wait(pe, xload, b, 16)
                wait(pe, mload, b, 144)
                for L in range(2):
                    ws = units(L)
                    if L == 0:
                        wait(pe, xT_ev, b, 0)
                        for m in range(2):
                            project(b, bank(2 * m), w0[:, 0], m, xc)
                            project(b, bank(2 * m + 1), w0[:, 1], m, xc)
                        project_rows(b, w0[:, 2], xc)
                        wait(pe, spread, b, 512)
                        wait(pe, v_ev, b, 2)
                    else:
                        wait(pe, x1, b, 2)
                        for m in range(2):
                            project(b, bank(m), w1[:, 0], m, xc)
                        project_rows(b, w1[:, 0], xc)
                        wait(pe, q_mask, b, 2)
                        wait(pe, v_ev, b, 4)
                    max_pass(b, ws[0], range(4))
                    max_transpose(b, ws[0])
                    for w in ws:
                        nxt = w + 1 if w + 1 in ws else None
                        wait(pe, nm_dma, b, 32 * (w + 1))
                        if nxt:
                            wait(pe, nm_row, b, w + 1)
                        for kc in range(KC):
                            scores(b, w, kc)
                            if kc == 0 and w > ws[0]:
                                finish(b, w - 1)
                            if nxt and kc < 2:
                                max_pass(b, nxt, (2 * kc,))
                            if kc:
                                values(b, w, kc - 1)
                            if nxt and kc < 2:
                                max_pass(b, nxt, (2 * kc + 1,))
                            if nxt and kc == 2:
                                max_transpose(b, nxt)
                        values(b, w, KC - 1)
                    finish(b, ws[-1])
                    wait(pe, yn, b, ws[-1] + 1)
                    for m in range(2):
                        for qb in range(KC):
                            last = pe.transpose(bank(m)[:, qb * P:(qb + 1) * P], yT[:, qb, m * P:(m + 1) * P], ident[:])
                        last.then_inc(back_mm.sem, 1)
                    if L == 1:
                        wait(pe, ctx_ev, b, 2)
                        for c in range(KC):
                            wait(pe, xT_ev, b, c - 1)
                            o = bank(2 + c % 2)
                            for k in range(2):
                                pe.matmul(o[:, 0:CH], raw2[:, k, c * P:(c + 1) * P], w1[:, 1, k, :], start=k == 0, stop=False, skip_group_check=True)
                            for k in range(2):
                                last = pe.matmul(o[:, k * P:(k + 1) * P], xc[:, k, c * P:(c + 1) * P], ident[:], start=False, stop=k == 1, skip_group_check=True)
                            last.then_inc(lo_mm.sem, 1)



def recurrent_and_last_layer(nc, xT, cond, w_ih, w_hh, b_ih, b_hh, b_row, wk, wo, rowc, cols, ident_in, out):
    fp32 = mybir.dt.float32
    ALU = mybir.AluOpType
    ACT = mybir.ActivationFunctionType
    AX = mybir.AxisListType
    P, C, T, B = xT.shape
    D = P * C
    GATES = 3
    TB = 64
    NB = 8
    RMS_EPS = 1e-6
    with ExitStack() as ctx:
        def sb(name, shape, dt=fp32):
            return ctx.enter_context(nc.sbuf_tensor(name, shape, dt))
        def pb(name, shape, dt=fp32):
            return ctx.enter_context(nc.psum_tensor(name, shape, dt))
        def sem(name):
            return ctx.enter_context(nc.semaphore(name))
        x2v = xT[:, :, :, :].rearrange("p c (i u) b -> p c i u b", u=2)
        hT = sb("hT", [P, 2, C, B])
        bT = sb("bT", [P, 2, GATES * C])
        bsum = sb("bsum", [P, GATES * C])
        bias_row = sb("bias_row", [P, D])
        one_row = sb("one_row", [P, B])
        trn = sb("trn", [P, GATES, P])
        tr = [trn[:, g, :].rearrange("p (c m) -> p c m", c=C)[:, :, 0:B] for g in range(GATES)]
        pre = sb("pre", [P, GATES, C, B])
        act = sb("act", [P, GATES, C, B])
        tmp = sb("tmp", [P, 3, C, B])
        ps = [pb(f"gate{g}", [P, 512]) for g in range(GATES)]
        pg = [pb(f"pg{g}", [P, 512]) for g in range(4)]
        (s_ld, s_wih, s_init, s_chain, s_zero, s_gi_mm, s_gi_ev, s_h, s_d, s_acc, s_out, s_free) = (
            sem("g_" + n) for n in "ld wih init chain zero gi_mm gi_ev h d acc out free".split())
        s_ps = [sem(f"s_ps{g}") for g in range(3)]
        s_tr = [sem(f"s_tr{g}") for g in range(3)]
        s_pre = [sem(f"s_pre{g}") for g in range(3)]
        s_act = [sem(f"s_act{g}") for g in range(3)]
        R, Z, N = 0, 1, 2
        NLD = 16 * 5
        MT = GATES * C
        gru = ctx.enter_context(ExitStack())
        giT = gru.enter_context(nc.sbuf_tensor("giT", [P, T, GATES * C * B], fp32))
        whh = gru.enter_context(nc.sbuf_tensor("whh", [P, C, GATES * D], fp32))
        gi4 = giT[:, :, :].rearrange("p t (g c b) -> p t g c b", g=GATES, c=C)
        gi2 = giT[:, :, :].rearrange("p (i u) (g c b) -> p i u g c b", u=2, g=GATES, c=C)
        with nc.sbuf_tensor("wih", [P, C, GATES * D], fp32) as wih, nc.Block() as block:
            @block.sync
            def _(sp):
                sp.dma_start(wih[:], w_ih).then_inc(s_ld, 16)
                sp.dma_start(bT[:, 0], b_ih).then_inc(s_ld, 16)
                sp.dma_start(bT[:, 1], b_hh).then_inc(s_ld, 16)
                sp.dma_start(hT[:, 0], cond).then_inc(s_ld, 16)
                sp.dma_start(whh[:], w_hh).then_inc(s_ld, 16)
                sp.wait_ge(s_zero, 3)
                sp.dma_start(bias_row[0:1, :], b_row).then_inc(s_wih, 16)

            @block.gpsimd
            def _(pool):
                pool.memset(bias_row[:], 0.0).then_inc(s_zero, 1)
                pool.memset(one_row[:], 0.0).then_inc(s_zero, 1)
                pool.wait_ge(s_zero, 2)
                pool.memset(one_row[0:1, :], 1.0).then_inc(s_zero, 1)
                pool.wait_ge(s_ld, NLD)
                pool.sem_inc(s_tr[N], 1)
                with pool.Fori(0, T // 2) as i:
                    for u in range(2):
                        pool.wait_ge(s_h, i * 2 + (u + 1))
                        xt = x2v[:, :, bass.ds(i, 1), u, :].rearrange("p c i b -> p c (i b)")
                        pool.tensor_tensor(xt, xt, hT[:, (u + 1) % 2, :, :], ALU.add).then_inc(s_acc, 1)

            @block.vector
            def _(dve):
                for g in range(3):
                    dve.memset(ps[g][:, 0:P], 0.0).then_inc(s_init, 1)
                dve.wait_ge(s_ld, NLD)
                dve.tensor_tensor(bsum[:, 0:2 * C], bT[:, 0, 0:2 * C], bT[:, 1, 0:2 * C], ALU.add).then_inc(s_init, 1)
                dve.tensor_copy(bsum[:, 2 * C:], bT[:, 0, 2 * C:]).then_inc(s_init, 1)
                dve.sem_inc(s_acc, 1)
                dve.wait_ge(s_gi_ev, 4 * MT)
                with dve.Fori(0, T // 2) as i:
                    for u in range(2):
                        t = i * 2
                        now = t + (u + 1)
                        h0, h1 = hT[:, u, :, :], hT[:, 1 - u, :, :]
                        def gi(g):
                            return gi2[:, bass.ds(i, 1), u, g, :, :].rearrange("p i c b -> p (i c) b")
                        dve.wait_ge(s_ps[R], now)
                        dve.transpose(trn[:, R, :], ps[R][:, 0:P]).then_inc(s_tr[R], 1)
                        dve.wait_ge(s_tr[R], now)
                        dve.tensor_tensor(pre[:, R], tr[R], gi(R), ALU.add).then_inc(s_pre[R], 1)
                        dve.wait_ge(s_ps[N], now)
                        dve.transpose(trn[:, N, :], ps[N][:, 0:P]).then_inc(s_tr[N], 1)
                        dve.wait_ge(s_tr[N], t + (u + 2))
                        dve.wait_ge(s_act[R], now)
                        dve.tensor_tensor(tmp[:, 0], tr[N], act[:, R], ALU.mult).then_inc(s_chain, 1)
                        dve.wait_ge(s_chain, t * 2 + (2 * u + 1))
                        dve.tensor_tensor(pre[:, N], tmp[:, 0], gi(N), ALU.add).then_inc(s_pre[N], 1)
                        dve.wait_ge(s_ps[Z], now)
                        dve.transpose(trn[:, Z, :], ps[Z][:, 0:P]).then_inc(s_tr[Z], 1)
                        dve.wait_ge(s_tr[Z], now)
                        dve.tensor_tensor(pre[:, Z], tr[Z], gi(Z), ALU.add).then_inc(s_pre[Z], 1)
                        dve.wait_ge(s_act[N], now)
                        dve.tensor_tensor(tmp[:, 1], h0, act[:, N], ALU.subtract).then_inc(s_d, 1)
                        dve.wait_ge(s_d, now)
                        dve.wait_ge(s_act[Z], now)
                        dve.tensor_tensor(tmp[:, 2], tmp[:, 1], act[:, Z], ALU.mult).then_inc(s_chain, 1)
                        dve.wait_ge(s_chain, t * 2 + (2 * u + 2))
                        dve.wait_ge(s_acc, t + (u + 1) if u == 0 else t + 2)
                        dve.tensor_tensor(h1, tmp[:, 2], act[:, N], ALU.add).then_inc(s_h, 1)

            @block.scalar
            def _(a):
                a.wait_ge(s_init, 5)
                for blk in range(4):
                    for m in range(MT):
                        n = blk * MT + m
                        a.wait_ge(s_gi_mm, n + 1)
                        a.activation(gi4[:, TB * blk:TB * (blk + 1), m // C, m % C, :],
                                     pg[n % 4][:, :].rearrange("p (t b) -> p t b", b=B),
                                     ACT.Identity, bias=bsum[:, m:m + 1]).then_inc(s_gi_ev, 1)
                with a.Fori(0, T // 2) as i:
                    for u in range(2):
                        for g, f in ((R, ACT.Sigmoid), (N, ACT.Tanh), (Z, ACT.Sigmoid)):
                            a.wait_ge(s_pre[g], i * 2 + (u + 1))
                            a.activation(act[:, g], pre[:, g], f).then_inc(s_act[g], 1)

            @block.tensor
            def _(pe):
                pe.wait_ge(s_ld, NLD)
                for blk in range(4):
                    for m in range(MT):
                        n = blk * MT + m
                        if n >= 4:
                            pe.wait_ge(s_gi_ev, n - 3)
                        for k in range(C):
                            last = pe.matmul(pg[n % 4][:, :], wih[:, k, m * P:(m + 1) * P],
                                             xT[:, k, TB * blk:TB * (blk + 1), :].rearrange("p t b -> p (t b)"), start=k == 0, stop=k == C - 1)
                        last.then_inc(s_gi_mm, 1)
                pe.wait_ge(s_zero, 3)
                pe.wait_ge(s_wih, 16)
                pe.wait_ge(s_init, 3)
                pe.sem_inc(s_free, 1)
                with pe.Fori(0, T // 2) as i:
                    for u in range(2):
                        t = i * 2
                        pe.wait_ge(s_tr[N], t + (u + 1))
                        for j in range(4):
                            pe.matmul(ps[N][32 * j:32 * j + B, 0:P], one_row[:, :], bias_row[:, P * j:P * (j + 1)], start=True, stop=False)
                        if u == 1:
                            pe.wait_ge(s_h, t + 1)
                        else:
                            pe.wait_ge(s_h, t) if False else pe.wait_ge(s_acc, t + 1)
                        for g in (R, N, Z):
                            for c in range(C):
                                for j in range(4):
                                    o = g * D + P * j
                                    last = pe.matmul(ps[g][32 * j:32 * j + B, 0:P], hT[:, u, c, :], whh[:, c, o:o + P],
                                                     start=c == 0 and g != N, stop=c == C - 1)
                            last.then_inc(s_ps[g], 1)
        gru.close()
        wkT = sb("wkT", [P, C, D]); woT = sb("woT", [P, C, D])
        ident = sb("identg", [P, P]); ones = sb("onesg", [P, P])
        rw = sb("rw", [64, 2, D])
        colv = sb("colv", [P, 2, C])
        br = sb("br", [P, C, NB, B])
        keys = sb("keys", [64, D]); kq = sb("kq", [64, D])
        st = sb("stt", [64, 8])
        row = sb("row", [1, 8, 64])
        attb = sb("attb", [P, NB * B])
        prod = sb("prod", [P, C, NB, B]); att = sb("att", [P, C, B]); pj = sb("pj", [P, C, B])
        eps = sb("eps", [P, 1])
        W5 = 512
        xa = sb("xa", [P, 2, C, W5]); sq = sb("sq", [P, 2, C, W5]); rs = sb("rs", [P, 2, W5])
        pm = [pb(f"pm{i}", [P, W5]) for i in range(1)]
        f_ld, f_v, f_pe, f_a, f_p, f_out = (sem("f_" + n) for n in "ld v pe a p out".split())
        f_x, f_mu, f_c, f_sq, f_var, f_sd, f_rs, f_n, f_gb = (sem("f2_" + n) for n in "x mu c sq var sd rs n gb".split())
        f_o2 = [sem(f"f_o{i}") for i in range(2)]
        KP, BP, MU, VA = ps[0], ps[1], pg[0:2], pg[2:4]
        with nc.Block() as block:
            @block.sync
            def _(sp):
                sp.dma_start(wkT[:], wk).then_inc(f_ld, 16)
                sp.dma_start(woT[:], wo).then_inc(f_ld, 16)
                sp.dma_start(ident[:], ident_in).then_inc(f_ld, 16)
                for i in range(2):
                    sp.dma_start(rw[:, i, :], rowc[i:i + 1, :].to_broadcast([64, D])).then_inc(f_ld, 16)
                sp.dma_start(colv[:], cols).then_inc(f_ld, 16)
                for blk in range(4):
                    sp.wait_ge(f_p, blk + 1)
                    sp.dma_start(out[:, :, TB * blk:TB * (blk + 1), :].rearrange("p c t b -> p c (t b)"), sq[:, blk % 2]).then_inc(f_o2[blk % 2], 16)
                for q in f_o2:
                    sp.wait_ge(q, 32)

            @block.vector
            def _(dve):
                k = [0]
                def link(ins):
                    k[0] += 1
                    ins.then_inc(f_v, 1)
                    dve.wait_ge(f_v, k[0])
                dve.memset(eps[:], RMS_EPS)
                dve.memset(ones[:], 1.0).then_inc(f_v, 1)
                k[0] = 1
                for c in range(C):
                    dve.tensor_reduce(br[:, c], xT[:, c, :, :].rearrange("p (n i) b -> p n b i", n=NB), AX.X, ALU.add).then_inc(f_v, 1)
                k[0] += C
                dve.wait_ge(f_pe, 1)
                link(dve.tensor_copy(keys[:], KP[0:64, :]))
                dve.wait_ge(f_ld, 96)
                link(dve.tensor_tensor(kq[:], keys[:], keys[:], ALU.mult))
                link(dve.reduce_sum(st[:, 0:1], kq[:], AX.X))
                link(dve.tensor_scalar(st[:, 1:2], st[:, 0:1], 1.0 / D, RMS_EPS, ALU.mult, ALU.add))
                dve.wait_ge(f_a, 1)
                link(dve.reciprocal(st[:, 3:4], st[:, 2:3]))
                link(dve.tensor_scalar(kq[:], keys[:], st[:, 3:4], None, ALU.mult))
                link(dve.tensor_tensor(keys[:], kq[:], rw[:, 0, :], ALU.mult))
                link(dve.tensor_tensor(kq[:], keys[:], rw[:, 1, :], ALU.mult))
                link(dve.reduce_sum(st[:, 4:5], kq[:], AX.X))
                V_SCORE = k[0]
                dve.wait_ge(f_pe, 2)
                r = [row[0:1, i, :].rearrange("p (n b) -> p n b", b=B) for i in range(8)]
                link(dve.tensor_copy(row[0:1, 0, :], BP[0:1, 0:64]))
                link(dve.reduce_max(row[0:1, 1, 0:B], r[0].rearrange("p n b -> p b n"), AX.X))
                bc = lambda i: row[0:1, i, 0:B].rearrange("p (a b) -> p a b", a=1).to_broadcast([1, NB, B])
                link(dve.tensor_tensor(r[2], r[0], bc(1), ALU.subtract))
                dve.wait_ge(f_a, 2)
                link(dve.reduce_sum(row[0:1, 4, 0:B], r[3].rearrange("p n b -> p b n"), AX.X))
                link(dve.reciprocal(row[0:1, 5, 0:B], row[0:1, 4, 0:B]))
                link(dve.tensor_tensor(r[6], r[3], bc(5), ALU.mult))
                dve.wait_ge(f_pe, 3)
                link(dve.tensor_copy(attb[:], KP[:, 0:64]))
                for c in range(C):
                    dve.tensor_tensor(prod[:, c], br[:, c], attb[:].rearrange("p (n b) -> p n b", b=B), ALU.mult).then_inc(f_v, 1)
                k[0] += C
                dve.wait_ge(f_v, k[0])
                for c in range(C):
                    dve.tensor_reduce(att[:, c], prod[:, c].rearrange("p n b -> p b n"), AX.X, ALU.add).then_inc(f_v, 1)
                k[0] += C
                assert (V_SCORE, k[0]) == (14, 29), (V_SCORE, k[0])
                dve.wait_ge(f_pe, 4)
                link(dve.tensor_copy(pj[:], BP[:, 0:C * B].rearrange("p (c b) -> p c b", c=C)))

                def centre(blk):
                    h = blk % 2
                    dve.wait_ge(f_mu, blk + 1)
                    for c in range(C):
                        dve.scalar_tensor_tensor(xa[:, h, c], MU[h][:, :], -1.0 / D, xa[:, h, c], ALU.mult, ALU.add).then_inc(f_c, 1)

                def shift(blk):
                    h = blk % 2
                    if blk >= 2:
                        dve.wait_ge(f_gb, 4 * (blk - 1))
                    for c in range(C):
                        dve.tensor_tensor(xa[:, h, c].rearrange("p (t b) -> p t b", b=B), xT[:, c, TB * blk:TB * (blk + 1), :],
                                          pj[:, c:c + 1, :].to_broadcast([P, TB, B]), ALU.add).then_inc(f_x, 1)

                def scale(blk):
                    h = blk % 2
                    dve.wait_ge(f_sd, blk + 1)
                    dve.reciprocal(rs[:, h], rs[:, h]).then_inc(f_rs, 1)
                    dve.wait_ge(f_rs, blk + 1)
                    dve.wait_ge(f_c, 4 * blk + 4)
                    for c in range(C):
                        dve.tensor_tensor(xa[:, h, c], xa[:, h, c], rs[:, h], ALU.mult).then_inc(f_n, 1)
                shift(0)
                for blk in range(4):
                    centre(blk)
                    if blk + 1 < 4:
                        shift(blk + 1)
                    scale(blk)

            @block.tensor
            def _(pe):
                pe.wait_ge(f_ld, 96)
                pe.wait_ge(f_v, 1 + C)
                for c in range(C):
                    last = pe.matmul(KP[0:64, :], br[:, c].rearrange("p n b -> p (n b)"), wkT[:, c, :], start=c == 0, stop=c == C - 1)
                last.then_inc(f_pe, 1)
                pe.wait_ge(f_v, 14)
                pe.matmul(BP[0:1, 0:64], st[:, 4:5], ident[0:64, 0:64], start=True, stop=True).then_inc(f_pe, 1)
                pe.wait_ge(f_v, 20)
                pe.matmul(KP[:, 0:64], ones[0:1, :], row[0:1, 6, :], start=True, stop=True).then_inc(f_pe, 1)
                pe.wait_ge(f_v, 29)
                for m in range(C):
                    for c in range(C):
                        last = pe.matmul(BP[:, m * B:(m + 1) * B], woT[:, c, m * P:(m + 1) * P], att[:, c, :], start=c == 0, stop=c == C - 1)
                last.then_inc(f_pe, 1)

                def mean(blk):
                    h = blk % 2
                    pe.wait_ge(f_x, 4 * blk + 4)
                    if blk >= 2:
                        pe.wait_ge(f_c, 4 * (blk - 1))
                    for c in range(C):
                        last = pe.matmul(MU[h][:, :], ones[:], xa[:, h, c], start=c == 0, stop=c == C - 1)
                    last.then_inc(f_mu, 1)

                def var(blk):
                    h = blk % 2
                    pe.wait_ge(f_sq, 4 * blk + 4)
                    if blk >= 2:
                        pe.wait_ge(f_sd, blk - 1)
                    for c in range(C):
                        last = pe.matmul(VA[h][:, :], ones[:], sq[:, h, c], start=c == 0, stop=c == C - 1)
                    last.then_inc(f_var, 1)
                for blk in range(4):
                    mean(blk)
                    var(blk)

            @block.scalar
            def _(a):
                a.wait_ge(f_v, 9)
                a.activation(st[:, 2:3], st[:, 1:2], ACT.Sqrt).then_inc(f_a, 1)
                a.wait_ge(f_v, 17)
                a.activation(row[0:1, 3, :], row[0:1, 2, :], ACT.Exp).then_inc(f_a, 1)
                for blk in range(4):
                    h = blk % 2
                    for c in range(C):
                        a.wait_ge(f_c, 4 * blk + c + 1)
                        if blk >= 2:
                            a.wait_ge(f_o2[h], 16 * (blk // 2))
                        a.activation(sq[:, h, c], xa[:, h, c], ACT.Square).then_inc(f_sq, 1)
                    a.wait_ge(f_var, blk + 1)
                    if blk >= 2:
                        a.wait_ge(f_n, 4 * (blk - 1))
                    a.activation(rs[:, h], VA[h][:, :], ACT.Sqrt, scale=1.0 / D, bias=eps[:, 0:1]).then_inc(f_sd, 1)
                    for c in range(C):
                        a.wait_ge(f_n, 4 * blk + c + 1)
                        a.activation(sq[:, h, c], xa[:, h, c], ACT.Identity, scale=colv[:, 0, c:c + 1], bias=colv[:, 1, c:c + 1]).then_inc(f_gb, 1)

            @block.gpsimd
            def _(pool):
                for blk in range(4):
                    h = blk % 2
                    pool.wait_ge(f_gb, 4 * blk + 4)
                    pool.tensor_tensor(sq[:, h], sq[:, h], xT[:, :, TB * blk:TB * (blk + 1), :].rearrange("p c t b -> p c (t b)"), ALU.add).then_inc(f_p, 1)


def gru_inputs(v, np):
    f = lambda w: w.reshape(4, 4, 32, -1).transpose(0, 2, 1, 3).reshape(128, 4, -1)
    cp = lambda w: w.reshape(w.shape[0], -1, 4, 4, 32).transpose(0, 1, 3, 2, 4).reshape(w.shape)
    bt = lambda b: b.reshape(3, 4, 4, 32).transpose(1, 3, 0, 2).reshape(128, 12)
    col = lambda b: b.reshape(4, 4, 32).transpose(0, 2, 1).reshape(128, 4)
    return dict(cond=f(v['cond_2048'].T), w_ih=f(cp(v['L2_cond_W_ih'])), w_hh=f(v['L2_cond_W_hh']),
                b_ih=bt(v['L2_cond_b_ih']), b_hh=bt(v['L2_cond_b_hh']), b_row=v['L2_cond_b_hh'][None, 1024:],
                wk=f(v['L3_cond_Wk'].T), wo=f(cp(v['L3_cond_Wo'].T)),
                rowc=np.stack([v['L3_cond_rms_weight'], v['cond_2048'][1]]),
                cols=np.stack([col(v['L3_cond_ln_gamma']), col(v['L3_cond_ln_beta'])], axis=1), ident=np.eye(128, dtype=np.float32))



ATTENTION = ("x", "mask", "wq0", "wk0", "wv0", "b0", "wq1", "wo1", "ident")
RECURRENT = ("cond", "w_ih", "w_hh", "b_ih", "b_hh", "b_row", "wk", "wo", "rowc", "cols", "ident")


def build(nc, d, out):
    B, T, D = 8, 256, 512
    with nc.sbuf_tensor("xT", [128, D // 128, T, B], mybir.dt.float32) as xT:
        attention_layers(nc, xT, *(d[n] for n in ATTENTION))
        recurrent_and_last_layer(nc, xT, *(d[n] for n in RECURRENT), out)


def kernel(**inputs):
    import numpy as _np
    import concourse.bacc as _bacc
    from concourse import mybir as _mybir
    from concourse.bass_utils import run_bass_kernel_spmd as _run

    nc = _bacc.Bacc("TRN2", target_bir_lowering=False, num_devices=1)
    v = {k: _np.asarray(a) for k, a in inputs.items()}
    wt = lambda a: a.T.reshape(2, 128, 256).transpose(1, 0, 2)
    perm = lambda a: a.reshape(a.shape[:-1] + (4, 4, 32)).swapaxes(-3, -2).reshape(a.shape)
    ins = dict(x=perm(v['x']).reshape(8, 2, 128, 512).transpose(2, 1, 0, 3), mask=perm(v['cond_2048']),
               wq0=wt(v['L0_cond_Wq']), wk0=wt(v['L0_cond_Wk']), wv0=wt(v['L0_cond_Wv']), b0=v['L0_cond_b'],
               wq1=wt(v['L1_cond_Wq']), wo1=wt(v['L1_cond_Wo']), **gru_inputs(v, _np))
    arrays, d = {}, {}
    for name, a in ins.items():
        a = _np.ascontiguousarray(a)
        arrays[f"in_{name}_dram"] = a
        d[name] = nc.dram_tensor(f"in_{name}_dram", a.shape, _mybir.dt.from_np(a.dtype), kind="ExternalInput").ap()
    out = nc.dram_tensor("out_0_dram", (128, 4, 256, 8), _mybir.dt.float32, kind="ExternalOutput").ap()
    build(nc, d, out)
    r = _run(nc, [arrays], core_ids=[0])
    y = r.results[0]["out_0_dram"]
    return y.reshape(4, 32, 4, 256, 8).transpose(4, 3, 0, 2, 1).reshape(8, 256, 512)
```

```python
import concourse.bass as bass
from concourse import mybir
from contextlib import ExitStack


def attention_layers(nc, xT, x, mask, wq0, wk0, wv0, b0, wq1, wo1, ident_in):
    fp32 = mybir.dt.float32
    bf16 = mybir.dt.bfloat16
    ALU = mybir.AluOpType
    ACT = mybir.ActivationFunctionType
    AX = mybir.AxisListType
    P = 128
    B, T = x.shape[2], x.shape[3]
    CH = x.shape[1] * P
    KC = T // P
    NEG = 1e30
    DH = (16, 32)
    SCALE = (1.0 / 4.0, float(1.0 / 32.0 ** 0.5))
    HEADS = (CH // DH[0], CH // DH[1])
    UNITS = [(0, g) for g in range(4)] + [(1, g) for g in range(2)]
    NU = len(UNITS)
    SLOTS = NU * KC
    LAST0, LAST1 = 3, 5
    OFF = [0 if L == 0 else -1 for L, g in UNITS]
    TERMS0 = [(0, 0), (0, 1), (1, 0), (1, 1), (0, 2), (2, 0), (1, 2)]
    TERMS1 = [[(0, 0), (0, 1), (1, 0)], [(1, 1), (0, 2), (2, 0), (1, 2)]]
    R0 = len(TERMS0) * DH[0]
    R1 = len(TERMS1[0]) * DH[1]
    with ExitStack() as ctx:
        def sb(name, shape, dt=fp32):
            return ctx.enter_context(nc.sbuf_tensor(name, shape, dt))

        def pb(name, shape, dt=fp32):
            return ctx.enter_context(nc.psum_tensor(name, shape, dt))

        def sem(name):
            return ctx.enter_context(nc.semaphore(name))

        def dram(name, shape, dt):
            return nc.dram_tensor(name, shape, dt, kind="Internal").ap()

        xin = sb("xin", [P, 2, T])
        x1 = sb("x1", [P, 2, T])
        w0 = sb("w0", [P, 3, 2, CH])
        w1 = sb("w1", [P, 2, 2, CH])
        ident = sb("ident", [P, P])
        ones = sb("ones", [P, 32])
        zero = sb("zero", [16, P])
        sel = sb("sel", [P, 4])
        K0 = sb("K0", [P, HEADS[0], T], bf16)
        Q0 = sb("Q0", [P, HEADS[0], T], bf16)
        K1 = [sb(f"K1{i}", [P, HEADS[1], T], bf16) for i in range(2)]
        Q1 = [sb(f"Q1{i}", [P, HEADS[1], T], bf16) for i in range(2)]
        SIDES = ("q0", "k0", "k1", "q1")
        full = {s: sb(f"full_{s}", [P, 2, T]) for s in SIDES}
        piece = {s: sb(f"piece_{s}", [P, 3, 2, T], bf16) for s in SIDES}
        va = sb("va", [P, KC, HEADS[0], 17])
        vb = sb("vb", [P, KC, CH])
        mbc = sb("mbc", [P, T])
        anyc = sb("anyc", [P, 1])
        mx = sb("mx", [P, NU, 16])
        nm = sb("nm", [16, NU, P])
        nmp = sb("nmp", [16, NU, 3, P], bf16)
        pr = sb("pr", [P, 2, 4, T])
        raw = sb("raw", [P, T])
        rawd = sb("rawd", [P, T])
        rd = sb("rd", [P, 16])
        yT = [sb(f"yT{L}", [P, KC, CH]) for L in range(2)]
        ctxs = sb("ctxs", [P, 2, T])
        m8, mb8, t8 = raw[0:B, :], rawd[0:B, :], ctxs[0:B, 0, :]
        any8, b8, br8 = sb("any8", [B, 1]), sb("b8", [B, 1]), sb("br8", [B, 2])
        rows8 = piece["q1"][0:B].rearrange("p j m t -> p (j m) t")
        d_any = dram("d_any", [B, 1], fp32)
        d_rows = dram("d_rows", [B, 6, T], bf16)
        d_piece = {s: dram(f"d_{s}", [3, DH[int(s[1])], HEADS[int(s[1])], T], bf16) for s in SIDES}
        MX = [pb(f"MX{i}", [P, T]) for i in range(2)]
        ST = pb("ST", [P, 4 * T])
        AV = pb("AV", [P, T])
        DN = pb("DN", [P, T])

        class Signal:
            def __init__(self, name, per):
                self.sem, self.per = sem(name), per

            def at(self, b, n):
                return b * self.per + n

        def each(name, per):
            return [Signal(f"{name}{w}", per) for w in range(NU)]

        weights, const, masks_in, masks_out = (sem(n) for n in ("weights", "const", "masks_in", "masks_out"))
        mx_mm, mx_red, mxT_mm, nm_row, nm_split, nm_dma = (each(n, k) for n, k in (
            ("mx_mm", 16), ("mx_red", 16), ("mxT_mm", 1), ("nm_row", 1), ("nm_split", 4), ("nm_dma", 48)))
        st_mm, exped, av_mm, raw_ev, fin_mm, rden, yn = (each(n, k) for n, k in (
            ("st_mm", 8), ("exped", 8), ("av_mm", 4), ("raw_ev", 1), ("fin_mm", 1), ("rden", 1), ("yn", 1)))
        rawd_ev, den_mm = ({w: Signal(f"{name}{w}", 1) for w in range(NU) if UNITS[w][0] == 1} for name in ("rawd_ev", "den_mm"))
        proj_mm = {s: Signal(f"proj_{s}", 2) for s in ("q0", "k0", "k1")}
        proj_ev = {s: Signal(f"projev_{s}", 2) for s in SIDES}
        split = {s: Signal(f"split_{s}", 4) for s in SIDES}
        piece_out = {s: Signal(f"pout_{s}", 96) for s in SIDES}
        stacked = [Signal("stacked0", 16 * (2 * len(TERMS0) + 2)), Signal("stacked1", 16 * (2 * 7 + 2))]
        v_mm = [Signal(f"v_mm{L}", 2) for L in range(2)]
        v_ev = [Signal(f"v_ev{L}", 2) for L in range(2)]
        back_mm = [Signal(f"back_mm{L}", 2) for L in range(2)]
        xin_in, xres_in, mbc_in = (Signal(n, k) for n, k in (("xin_in", 32), ("xres_in", 16), ("mbc_in", 16)))
        x1_sum, x1T_mm, x1T_ev, ctx_ev, lo_mm, xT_sum = (Signal(n, 2) for n in ("x1_sum", "x1T_mm", "x1T_ev", "ctx_ev", "lo_mm", "xT_sum"))

        gate = sem("gate")
        apart = []

        def there(b):
            return not isinstance(b, int) or 0 <= b < B

        def wait(eng, signal, b, n):
            if there(b):
                if any(eng is e for e in apart):
                    eng.wait_ge(const, 1)
                eng.wait_ge(signal.sem, signal.at(b, n))

        LEAD = {w: 6 for w in range(NU)}
        LEAD[0] = 3

        def at_slot(s):
            w, kc = divmod(s, KC)
            maxima = []
            for u in range(NU):
                for qb in range(KC):
                    t = KC * u - LEAD[u] + (qb if LEAD[u] > 3 else max(qb - 1, 0))
                    if t % SLOTS == s:
                        maxima.append((u, qb, OFF[u] + (1 if t < 0 else 0)))
            turns = [("max", (u, qb, i), o) for u, qb, o in maxima for i in range(4)]
            steps = turns[:len(turns) // 2]
            steps.append(("score", (w, kc), OFF[w]))
            if s % KC == 1:
                u = (w - 1) % NU
                steps.append(("finish", (u,), OFF[u] - (1 if w == 0 else 0)))
            extra = {0: [("proj", ("k1",), -1), ("split", (1,), -1)], 2: [("values", (1,), -1), ("back", (1,), -2)], 3: [("out", (), -2)],
                     10: [("proj", ("q0",), 1)], 11: [("proj", ("k0",), 1)], 12: [("split", (0,), 1)],
                     17: [("values", (0,), 1)], 18: [("back", (0,), 0)], 19: [("x1T", (), 0)]}
            steps += extra.get(s, [])
            steps += turns[len(turns) // 2:]
            pw, pk = divmod((s - 1) % SLOTS, KC)
            steps.append(("av", (pw, pk), OFF[pw] - (1 if s == 0 else 0)))
            steps += [("maxT", (u,), o) for u, qb, o in maxima if qb == KC - 1]
            return steps

        def jobs_of(name, a):
            if name == "max":
                u, qb, i = a
                return [(mx_red[u], 4 * qb + i + 1)]
            if name == "maxT":
                return [(nm_row[a[0]], 1)]
            if name == "finish":
                return [(rden[a[0]], 1), (yn[a[0]], 1)] if UNITS[a[0]][0] else [(yn[a[0]], 1)]
            if name == "proj":
                return [(proj_ev[a[0]], m + 1) for m in range(2)]
            if name == "values":
                return [(v_ev[a[0]], m + 1) for m in range(2)]
            if name == "back":
                return [((x1_sum, ctx_ev)[a[0]], m + 1) for m in range(2)]
            if name == "x1T":
                return [(x1T_ev, m + 1) for m in range(2)]
            if name == "out":
                return [(xT_sum, m + 1) for m in range(2)]
            return []

        PLAN = [at_slot(s) for s in range(SLOTS)]
        LOOP = (2, B - 1)
        ITS = [-1, 0, 1, None] + [B - 1, B, B + 1]
        SHOWN = {None: LOOP[0]}
        parity, first_bank = 0, {}
        for it in ITS:
            first_bank[it] = parity
            n = sum(len(jobs_of(name, a)) for step in PLAN for name, a, o in step if there(SHOWN.get(it, it) + o))
            parity = (parity + n) % 2
            assert it is not None or n % 2 == 0

        class Walk:
            def __init__(self, eng):
                self.eng, self.round, self.it = eng, 0, None
                self.readers = [None, None]
                self.past = {"score": [], "av": []}

            def batch(self, off, round_):
                return self.it + (off - (self.round - round_))

            def ago(self, name, k):
                past = self.past[name]
                if len(past) <= k:
                    return None
                w, kc, off, round_ = past[-1 - k]
                return w, kc, self.batch(off, round_)

            def clear(self, j):
                if self.priors[j] is not None:
                    signal, n, off, round_ = self.priors[j]
                    wait(self.eng, signal, self.batch(off, round_), n)

            def iteration(self, key, it, handlers):
                self.round += 1
                self.it = it
                bank = first_bank[key]
                for name, a, o in (step for steps in PLAN for step in steps):
                    if not there(SHOWN.get(key, it) + o):
                        continue
                    self.priors, self.banks = [], []
                    for j, (signal, n) in enumerate(jobs_of(name, a)):
                        i = (bank + j) % 2
                        self.banks.append(MX[i])
                        self.priors.append(self.readers[i])
                        self.readers[i] = (signal, n, o, self.round)
                    bank += len(self.banks)
                    if name in self.past:
                        self.past[name].append((*a, o, self.round))
                    if name in handlers:
                        handlers[name](it + o, self.banks, *a)

            def run(self, handlers):
                for key in ITS:
                    if key is None:
                        with self.eng.Fori(*LOOP) as it:
                            self.iteration(None, it, handlers)
                    else:
                        self.iteration(key, key, handlers)
        CONST = 11
        block = ctx.enter_context(nc.Block())

        @block.sync
        def _(sp):
            apart.append(sp)
            sp.dma_start(m8[:], mask).then_inc(masks_in, 16)
            sp.dma_start(b8[:], b0.rearrange("(a n) -> a n", a=1).to_broadcast([B, 1])).then_inc(masks_in, 16)
            for i, d in enumerate((wq0, wk0, wv0)):
                sp.dma_start(w0[:, i], d).then_inc(weights, 16)
            for i, d in enumerate((wq1, wo1)):
                sp.dma_start(w1[:, i], d).then_inc(weights, 16)
            sp.dma_start(ident[:], ident_in).then_inc(weights, 16)
            sp.wait_ge(masks_out, 12)
            sp.dma_start(d_any, any8[:]).then_inc(masks_in, 16)
            sp.dma_start(d_rows, rows8[:]).then_inc(masks_in, 16)
            sp.wait_ge(masks_in, 64)
            sp.wait_ge(const, CONST)

            def row(b):
                return bass.ds(b, 1)

            def pieces(b, s):
                for j, n in ((0, 1), (1, 3), (2, 4)):
                    wait(sp, split[s], b, n)
                    for m in range(2):
                        to = d_piece[s][j].rearrange("d (m h) t -> m h d t", m=2)[m]
                        sp.dma_start(to, piece[s][:, j, m]).then_inc(piece_out[s].sem, 16)

            def load_mask(b):
                wait(sp, proj_ev["q1"], b - 1, 2)
                sp.dma_start(mbc[:], mask[row(b), :].to_broadcast([P, T])).then_inc(mbc_in.sem, 16)

            def load_res(b):
                wait(sp, v_mm[1], b - 1, 2)
                sp.dma_start(x1[:], x[:, :, row(b), :].rearrange("p k b t -> p k (b t)")).then_inc(xres_in.sem, 16)

            def load_in(b):
                wait(sp, v_mm[0], b - 1, 2)
                sp.dma_start(xin[:], x[:, :, row(b), :].rearrange("p k b t -> p k (b t)")).then_inc(xin_in.sem, 16)
                wait(sp, proj_ev["q0"], b - 1, 2)
                sp.dma_start(anyc[:], d_any[row(b), :].to_broadcast([P, 1])).then_inc(xin_in.sem, 16)

            def stack(b, L):
                names = (("q0", "k0"), ("k1", "q1"))[L]
                for s in names:
                    pieces(b, s)
                for s in names:
                    wait(sp, piece_out[s], b, 96)
                wait(sp, st_mm[(LAST0, LAST1)[L]], b - 1, 8)
                for s in names:
                    side = 0 if s[0] == "k" else 1
                    if L == 0:
                        for t, pair in enumerate(TERMS0):
                            sp.dma_start((K0, Q0)[side][16 * t:16 * t + 16, :, :],
                                         d_piece[s][pair[side]]).then_inc(stacked[0].sem, 16)
                    else:
                        for part in range(2):
                            for t, pair in enumerate(TERMS1[part]):
                                sp.dma_start((K1, Q1)[side][part][32 * t:32 * t + 32, :, :],
                                             d_piece[s][pair[side]]).then_inc(stacked[1].sem, 16)
                H = HEADS[L]
                if L == 0:
                    sp.dma_start(K0[R0:R0 + 4, :, :], d_rows[row(b), 0:4, :].rearrange("b r t -> (b r) t").rearrange("r (a t) -> r a t", a=1).to_broadcast([4, H, T])).then_inc(stacked[0].sem, 16)
                    sp.dma_start(Q0[R0:R0 + 4, :, :], d_rows[row(b), 4:5, :].to_broadcast([4, H, T])).then_inc(stacked[0].sem, 16)
                else:
                    sp.dma_start(K1[0][R1:R1 + 1, :, :], d_rows[row(b), 0:1, :].to_broadcast([1, H, T])).then_inc(stacked[1].sem, 16)
                    sp.dma_start(Q1[0][R1:R1 + 1, :, :], d_rows[row(b), 5:6, :].to_broadcast([1, H, T])).then_inc(stacked[1].sem, 16)

            def iteration(key, it):
                k = SHOWN.get(key, it)
                if there(k - 1):
                    load_mask(it - 1)
                    stack(it - 1, 1)
                if there(k):
                    load_res(it)
                if there(k + 1):
                    load_in(it + 1)
                    stack(it + 1, 0)
            for key in ITS:
                if key is None:
                    with sp.Fori(*LOOP) as it:
                        iteration(None, it)
                else:
                    iteration(key, key)

        @block.gpsimd
        def _(pool):
            for buf in (ones, K0, Q0, K1[0], Q1[0], va):
                pool.memset(buf[:], 1.0).then_inc(const, 1)
            pool.memset(zero[:], 0.0).then_inc(const, 1)
            pool.wait_ge(weights, 96)
            pool.tensor_copy(sel[:], ident[:, 0:97:32]).then_inc(const, 1)

            def split_row(b, banks, u):
                L, g = UNITS[u]
                wait(pool, nm_row[u], b, 1)
                sig = nm_split[u]
                pool.tensor_tensor(nmp[:, u, 0], nm[:, u], zero[:], ALU.add).then_inc(sig.sem, 1)
                wait(pool, sig, b, 1)
                pool.tensor_tensor(nm[:, u], nm[:, u], nmp[:, u, 0], ALU.subtract).then_inc(sig.sem, 1)
                wait(pool, sig, b, 2)
                pool.tensor_tensor(nmp[:, u, 1], nm[:, u], zero[:], ALU.add).then_inc(sig.sem, 1)
                wait(pool, sig, b, 3)
                pool.tensor_tensor(nmp[:, u, 2], nm[:, u], nmp[:, u, 1], ALU.subtract).then_inc(sig.sem, 1)
                wait(pool, sig, b, 4)
                pool.sem_inc(gate, 1)
                dst, r = (Q0, R0 + 4) if L == 0 else (Q1[0], R1 + 1)
                for j in range(3):
                    pool.dma_start(dst[r + j:r + j + 1, 4 * g:4 * g + 4, :].rearrange("r h t -> r (h t)"), nmp[:, u, j]).then_inc(nm_dma[u].sem, 16)

            def split_(b, banks, L):
                sides = (("q0", "k0"), ("k1", "q1"))[L]
                for s in sides:
                    if s == "k1":
                        wait(pool, proj_ev["q1"], b, 2)
                    wait(pool, split[s], b, 1)
                    pool.tensor_tensor(full[s][:], full[s][:], piece[s][:, 0], ALU.subtract).then_inc(split[s].sem, 1)
                for s in sides:
                    wait(pool, split[s], b, 3)
                    pool.tensor_tensor(piece[s][:, 2], full[s][:], piece[s][:, 1], ALU.subtract).then_inc(split[s].sem, 1)
            pool.wait_ge(const, CONST)
            Walk(pool).run(dict(maxT=split_row, split=split_))

        @block.vector
        def _(dve):
            dve.memset(AV[:], 0.0).then_inc(const, 1)
            dve.memset(DN[:], 0.0).then_inc(const, 1)
            dve.memset(MX[0][:], 0.0).then_inc(const, 1)
            mo = masks_out
            dve.wait_ge(masks_in, 32)
            dve.reduce_max(any8[:], m8[:], AX.X).then_inc(mo, 1)
            dve.tensor_scalar(mb8[:], m8[:], NEG, -NEG, ALU.mult, ALU.add).then_inc(mo, 1)
            dve.tensor_scalar(b8[:], b8[:], 1.0 / SCALE[0], None, ALU.mult).then_inc(mo, 1)
            dve.tensor_copy(rows8[:, 5], m8[:]).then_inc(mo, 1)
            dve.wait_ge(mo, 3)
            dve.tensor_copy(rows8[:, 0], mb8[:]).then_inc(mo, 1)
            dve.tensor_scalar(rows8[:, 4], m8[:], 0.0, any8[:, 0:1], ALU.mult, ALU.add).then_inc(mo, 1)
            dve.tensor_scalar(t8[:], m8[:], 0.0, b8[:, 0:1], ALU.mult, ALU.add).then_inc(mo, 1)
            dve.wait_ge(mo, 7)
            dve.tensor_copy(rows8[:, 1], t8[:]).then_inc(mo, 1)
            dve.wait_ge(mo, 8)
            dve.tensor_tensor(t8[:], t8[:], rows8[:, 1], ALU.subtract).then_inc(mo, 1)
            dve.wait_ge(mo, 9)
            dve.tensor_copy(rows8[:, 2], t8[:]).then_inc(mo, 1)
            dve.wait_ge(mo, 10)
            dve.tensor_tensor(rows8[:, 3], t8[:], rows8[:, 2], ALU.subtract).then_inc(mo, 2)

            def max_(b, banks, u, qb, i):
                wait(dve, mx_mm[u], b, 4 * qb + i + 1)
                dve.reduce_max(mx[:, u, 4 * i + qb:4 * i + qb + 1], banks[0][:, :], AX.X).then_inc(mx_red[u].sem, 1)

            def finish(b, banks, u):
                L, g = UNITS[u]
                dh = DH[L]
                y = banks[-1][:, :].rearrange("p (q i d) -> p q i d", q=KC, i=4)
                if L == 0:
                    wait(dve, fin_mm[u], b, 1)
                    den = y[:, :, :, 16]
                else:
                    wait(dve, den_mm[u], b, 1)
                    den = banks[0][:, 0:16].rearrange("p (q i) -> p q i", q=KC)
                before = (b - 2, LAST1) if u == 0 else (b + 1, u - 1) if u == 4 else (b, u - 1)
                wait(dve, yn[before[1]], before[0], 1)
                dve.reciprocal(rd[:].rearrange("p (q i) -> p q i", q=KC), den).then_inc(rden[u].sem, 1)
                wait(dve, rden[u], b, 1)
                wait(dve, fin_mm[u], b, 1)
                for qb in range(KC):
                    last = dve.tensor_tensor(
                        yT[L][:, qb, 4 * dh * g:4 * dh * (g + 1)].rearrange("p (i d) -> p i d", i=4), y[:, qb, :, 0:dh],
                        rd[:, 4 * qb:4 * qb + 4].rearrange("p (i a) -> p i a", a=1).to_broadcast([P, 4, dh]), ALU.mult)
                last.then_inc(yn[u].sem, 1)

            def values(b, banks, L):
                for m in range(2):
                    wait(dve, v_mm[L], b, m + 1)
                    if m == 0:
                        wait(dve, av_mm[(LAST0, LAST1)[L]], b - 1, KC)
                    o = (va[:, 2 * m:2 * m + 2, :, 0:16] if L == 0 else vb[:, 2 * m:2 * m + 2, :])
                    i = banks[m][:, :].rearrange("p (k h d) -> p k h d", k=2, h=16) if L == 0 else banks[m][:, :].rearrange("p (k h) -> p k h", k=2)
                    dve.tensor_copy(o, i).then_inc(v_ev[L].sem, 1)

            def proj(b, banks, s):
                if s == "k1":
                    wait(dve, mbc_in, b, 16)
                    for m in range(2):
                        wait(dve, proj_ev["k1"], b, m + 1)
                        dve.tensor_tensor(full["q1"][:, m], full["k1"][:, m], mbc[:], ALU.mult).then_inc(proj_ev["q1"].sem, 1)

            def back(b, banks, L):
                if L == 0:
                    wait(dve, xres_in, b, 16)
                    for m in range(2):
                        wait(dve, back_mm[0], b, m + 1)
                        dve.tensor_tensor(x1[:, m], x1[:, m], banks[m][:, :], ALU.add).then_inc(x1_sum.sem, 1)

            def out_(b, banks):
                for m in range(2):
                    wait(dve, lo_mm, b, m + 1)
                    wait(dve, x1T_ev, b, 2)
                    o = xT[:, 2 * m:2 * m + 2, :, bass.ds(b, 1)].rearrange("p c o b -> p c (o b)")
                    dve.tensor_tensor(o, o, banks[m][:, :].rearrange("p (c o) -> p c o", c=2), ALU.add).then_inc(xT_sum.sem, 1)
            dve.wait_ge(const, CONST)
            Walk(dve).run({"max": max_, "finish": finish, "values": values, "proj": proj, "back": back, "out": out_})

        @block.scalar
        def _(act):
            def score(b, banks, w, kc):
                before = walk.ago("score", 2)
                if before:
                    u, k, bu = before
                    wait(act, av_mm[u], bu, k + 1)
                for p in range(2):
                    wait(act, st_mm[w], b, 2 * kc + p + 1)
                    act.activation(pr[:, kc % 2, 2 * p:2 * p + 2, :], ST[:, 2 * p * T:(2 * p + 2) * T].rearrange("p (a t) -> p a t", a=2),
                                   ACT.Exp, scale=SCALE[UNITS[w][0]]).then_inc(exped[w].sem, 1)

            def av(b, banks, w, kc):
                if kc != KC - 1:
                    return
                before = walk.ago("av", KC)
                if before:
                    wait(act, fin_mm[before[0]], before[2], 1)
                wait(act, av_mm[w], b, KC)
                act.copy(raw[:], AV[:, :]).then_inc(raw_ev[w].sem, 1)
                if UNITS[w][0] == 1:
                    act.copy(rawd[:], DN[:, :]).then_inc(rawd_ev[w].sem, 1)

            def max_row(b, banks, u):
                wait(act, mxT_mm[u], b, 1)
                act.activation(nm[:, u], banks[0][0:16, 0:P], ACT.Copy, scale=-1.0).then_inc(nm_row[u].sem, 1)

            def proj(b, banks, s):
                for m in range(2):
                    wait(act, proj_mm[s], b, m + 1)
                    if s == "q0":
                        wait(act, xin_in, b, 32)
                        act.activation(full[s][:, m], banks[m][:, :], ACT.Copy, scale=anyc[:, 0:1]).then_inc(proj_ev[s].sem, 1)
                    else:
                        act.copy(full[s][:, m], banks[m][:, :]).then_inc(proj_ev[s].sem, 1)

            def x1T(b, banks):
                for m in range(2):
                    wait(act, x1T_mm, b, m + 1)
                    o = xT[:, 2 * m:2 * m + 2, :, bass.ds(b, 1)].rearrange("p c o b -> p c (o b)")
                    act.copy(o, banks[m][:, :].rearrange("p (c o) -> p c o", c=2)).then_inc(x1T_ev.sem, 1)

            def back(b, banks, L):
                if L == 1:
                    for m in range(2):
                        wait(act, back_mm[1], b, m + 1)
                        act.copy(ctxs[:, m], banks[m][:, :]).then_inc(ctx_ev.sem, 1)

            def split_(b, banks, L):
                sides = (("q0", "k0"), ("k1", "q1"))[L]
                for s in sides:
                    wait(act, proj_ev[s], b, 2)
                    act.copy(piece[s][:, 0], full[s][:]).then_inc(split[s].sem, 1)
                for s in sides:
                    wait(act, split[s], b, 2)
                    act.copy(piece[s][:, 1], full[s][:]).then_inc(split[s].sem, 1)
            walk = Walk(act)
            walk.run({"score": score, "av": av, "maxT": max_row, "proj": proj, "x1T": x1T, "back": back, "split": split_})

        @block.tensor
        def _(pe):
            def tok(c):
                return slice(c * P, (c + 1) * P)

            def max_(b, banks, u, qb, i):
                L, g = UNITS[u]
                if qb == 0 and i == 0:
                    wait(pe, stacked[L], b, stacked[L].per)
                walk.clear(0)
                h = 4 * g + i
                k, q, r = (K0, Q0, R0 + 4) if L == 0 else (K1[0], Q1[0], R1 + 1)
                pe.matmul(banks[0][:, :], q[0:r, h, tok(qb)], k[0:r, h, :], start=True, stop=True).then_inc(mx_mm[u].sem, 1)

            def max_t(b, banks, u):
                wait(pe, mx_red[u], b, 16)
                walk.clear(0)
                pe.matmul(banks[0][0:16, 0:P], mx[:, u, :], ident[:], start=True, stop=True).then_inc(mxT_mm[u].sem, 1)

            def score(b, banks, w, kc):
                L, g = UNITS[w]
                if kc == 0:
                    wait(pe, nm_dma[w], b, 48)
                before = walk.ago("score", 1)
                for i in range(4):
                    if before and i % 2 == 0:
                        wait(pe, exped[before[0]], before[2], 2 * before[1] + i // 2 + 1)
                    o = ST[:, i * T:(i + 1) * T]
                    h = 4 * g + i
                    if L == 0:
                        last = pe.matmul(o, K0[0:R0 + 7, h, tok(kc)], Q0[0:R0 + 7, h, :], start=True, stop=True)
                    else:
                        pe.matmul(o, K1[0][0:R1 + 4, h, tok(kc)], Q1[0][0:R1 + 4, h, :], start=True, stop=False)
                        last = pe.matmul(o, K1[1][:, h, tok(kc)], Q1[1][:, h, :], start=False, stop=True)
                    if i % 2:
                        last.then_inc(st_mm[w].sem, 1)

            def av(b, banks, w, kc):
                L, g = UNITS[w]
                if kc == 0:
                    before = walk.ago("av", 1)
                    if before:
                        wait(pe, raw_ev[before[0]], before[2], 1)
                    if w == LAST1 - 1 and dn_used[0]:
                        wait(pe, rawd_ev[LAST1], b - 1, 1)
                    if w == LAST1:
                        wait(pe, rawd_ev[LAST1 - 1], b, 1)
                    if L == 1:
                        dn_used[0] = True
                    wait(pe, v_ev[L], b, 2)
                wait(pe, exped[w], b, 2 * kc + 2)
                for i in range(4):
                    h = 4 * g + i
                    r = slice(32 * i, 32 * i + (17 if L == 0 else 32))
                    v = va[:, kc, h, :] if L == 0 else vb[:, kc, 32 * h:32 * h + 32]
                    last = pe.matmul(AV[r, :], v, pr[:, kc % 2, i, :], start=kc == 0, stop=kc == KC - 1)
                if L == 1:
                    for i in range(4):
                        last = pe.matmul(DN[32 * i:32 * i + 32, :], ones[:], pr[:, kc % 2, i, :], start=kc == 0, stop=kc == KC - 1)
                last.then_inc(av_mm[w].sem, 1)
            dn_used = [False]

            def finish(b, banks, u):
                wait(pe, raw_ev[u], b, 1)
                if UNITS[u][0] == 1:
                    wait(pe, rawd_ev[u], b, 1)
                    walk.clear(0)
                    for qb in range(KC):
                        last = pe.matmul(banks[0][:, 4 * qb:4 * qb + 4], rawd[:, tok(qb)], sel[:], start=True, stop=True)
                    last.then_inc(den_mm[u].sem, 1)
                walk.clear(len(banks) - 1)
                for qb in range(KC):
                    last = pe.transpose(banks[-1][:, tok(qb)], raw[:, tok(qb)], ident[:])
                last.then_inc(fin_mm[u].sem, 1)

            def proj(b, banks, s):
                w_, src = (w1[:, 0], x1) if s == "k1" else (w0[:, 0 if s == "q0" else 1], xin)
                wait(pe, *((x1_sum, b, 2) if s == "k1" else (xin_in, b, 32)))
                for m in range(2):
                    walk.clear(m)
                    for k in range(2):
                        last = pe.matmul(banks[m][:, :], w_[:, k, m * P:(m + 1) * P], src[:, k, :], start=k == 0, stop=k == 1)
                    last.then_inc(proj_mm[s].sem, 1)

            def values(b, banks, L):
                w_, src = (w0[:, 2], xin) if L == 0 else (w1[:, 0], x1)
                for m in range(2):
                    walk.clear(m)
                    for h in range(2):
                        for k in range(2):
                            last = pe.matmul(banks[m][:, h * CH:(h + 1) * CH], src[:, k, tok(2 * m + h)], w_[:, k, :], start=k == 0, stop=k == 1)
                    last.then_inc(v_mm[L].sem, 1)

            def back(b, banks, L):
                wait(pe, yn[(LAST0, LAST1)[L]], b, 1)
                for m in range(2):
                    walk.clear(m)
                    for qb in range(KC):
                        last = pe.transpose(banks[m][:, tok(qb)], yT[L][:, qb, m * P:(m + 1) * P], ident[:])
                    last.then_inc(back_mm[L].sem, 1)

            def x1T(b, banks):
                wait(pe, x1_sum, b, 2)
                for m in range(2):
                    walk.clear(m)
                    for h in range(2):
                        for k in range(2):
                            last = pe.transpose(banks[m][:, h * CH + k * P:h * CH + (k + 1) * P], x1[:, k, tok(2 * m + h)], ident[:])
                    last.then_inc(x1T_mm.sem, 1)

            def out_(b, banks):
                wait(pe, ctx_ev, b, 2)
                for m in range(2):
                    walk.clear(m)
                    for h in range(2):
                        for k in range(2):
                            last = pe.matmul(banks[m][:, h * CH:(h + 1) * CH], ctxs[:, k, tok(2 * m + h)], w1[:, 1, k, :], start=k == 0, stop=k == 1)
                    last.then_inc(lo_mm.sem, 1)

            pe.wait_ge(weights, 96)
            pe.wait_ge(const, CONST)
            walk = Walk(pe)
            walk.run({"max": max_, "maxT": max_t, "score": score, "av": av, "finish": finish, "proj": proj,
                      "values": values, "back": back, "x1T": x1T, "out": out_})

def recurrent_and_last_layer(nc, xT, cond, w_ih, w_hh, b_ih, b_hh, wk, wo, rowc, cols, ident_in, out):
    fp32 = mybir.dt.float32
    ALU = mybir.AluOpType
    ACT = mybir.ActivationFunctionType
    AX = mybir.AxisListType
    P, C, T, B = xT.shape
    D = P * C
    GATES = 3
    TB = 64
    NB = 8
    RMS_EPS = 1e-6
    with ExitStack() as ctx:
        def sb(name, shape, dt=fp32):
            return ctx.enter_context(nc.sbuf_tensor(name, shape, dt))
        def pb(name, shape, dt=fp32):
            return ctx.enter_context(nc.psum_tensor(name, shape, dt))
        def sem(name):
            return ctx.enter_context(nc.semaphore(name))
        x2v = xT[:, :, :, :].rearrange("p c (i u) b -> p c i u b", u=2)
        giz = sb("giz", [P, 2, C, B])
        identz = sb("identz", [P, P])
        hT = sb("hT", [P, 2, C, B])
        bT = sb("bT", [P, 2, GATES * C])
        bsum = sb("bsum", [P, GATES * C])
        rbias = sb("rbias", [P, 2, 2, C, B])
        trn = sb("trn", [P, GATES, P])
        tr = [trn[:, g, :].rearrange("p (c m) -> p c m", c=C)[:, :, 0:B] for g in range(GATES)]
        pre = sb("pre", [P, GATES, C, B])
        act = sb("act", [P, GATES, C, B])
        tmp = sb("tmp", [P, 3, C, B])
        ps = [pb(f"gate{g}", [P, 512]) for g in range(GATES)]
        pg = [pb(f"pg{g}", [P, 512]) for g in range(4)]
        (s_ld, s_init, s_chain, s_rb, s_gi_mm, s_gi_ev, s_h, s_acc, s_giz) = (
            sem(n) for n in ("gru_loaded", "gates_cleared", "step_product", "bias_gated", "gi_products",
                             "gi_ready", "state_ready", "state_added", "giz_ready"))
        s_ps = [sem(f"gate_products{g}") for g in range(GATES)]
        s_tr = [sem(f"gate_turned{g}") for g in range(GATES)]
        s_pre = [sem(f"gate_summed{g}") for g in range(GATES)]
        s_act = [sem(f"gate_ready{g}") for g in range(GATES)]
        R, Z, N = 0, 1, 2
        NLD = 16 * 6
        MT = GATES * C
        gru = ctx.enter_context(ExitStack())
        giT = gru.enter_context(nc.sbuf_tensor("giT", [P, T + 2, GATES * C * B], fp32))
        whh = gru.enter_context(nc.sbuf_tensor("whh", [P, C, GATES * D], fp32))
        gi4 = giT[:, :, :].rearrange("p t (g c b) -> p t g c b", g=GATES, c=C)
        gi2 = giT[:, :, :].rearrange("p (i u) (g c b) -> p i u g c b", u=2, g=GATES, c=C)
        with nc.sbuf_tensor("wih", [P, C, GATES * D], fp32) as wih, nc.Block() as block:
            @block.sync
            def _(sp):
                sp.dma_start(wih[:], w_ih).then_inc(s_ld, 16)
                sp.dma_start(bT[:, 0], b_ih).then_inc(s_ld, 16)
                sp.dma_start(bT[:, 1], b_hh).then_inc(s_ld, 16)
                sp.dma_start(hT[:, 0], cond).then_inc(s_ld, 16)
                sp.dma_start(whh[:], w_hh).then_inc(s_ld, 16)
                sp.dma_start(identz[:], ident_in).then_inc(s_ld, 16)

            @block.gpsimd
            def _(pool):
                pool.wait_ge(s_ld, NLD)
                pool.sem_inc(s_tr[N], 1)
                pool.sem_inc(s_tr[Z], 1)
                bias_n = bT[:, 1, 2 * C:].rearrange("p (c a) -> p c a", a=1).to_broadcast([P, C, B])
                with pool.Fori(0, T // 2) as i:
                    for u in range(2):
                        pool.wait_ge(s_act[R], i * 2 + (u + 1))
                        pool.tensor_tensor(rbias[:, u, 0], act[:, R], bias_n, ALU.mult).then_inc(s_rb, 1)
                        pool.wait_ge(s_rb, i * 4 + (2 * u + 1))
                        pool.tensor_tensor(rbias[:, u, 1], rbias[:, u, 0], gi2[:, bass.ds(i, 1), u, N, :, :].rearrange("p i c b -> p (i c) b"), ALU.add).then_inc(s_rb, 1)
                        pool.wait_ge(s_h, i * 2 + (u + 1))
                        xt = x2v[:, :, bass.ds(i, 1), u, :].rearrange("p c i b -> p c (i b)")
                        pool.tensor_tensor(xt, xt, hT[:, (u + 1) % 2, :, :], ALU.add).then_inc(s_acc, 1)

            @block.vector
            def _(dve):
                dve.memset(giT[:, T:T + 2, :], 0.0).then_inc(s_init, 1)
                for g in range(3):
                    dve.memset(ps[g][:, 0:P], 0.0).then_inc(s_init, 1)
                dve.wait_ge(s_ld, NLD)
                dve.tensor_tensor(bsum[:, 0:2 * C], bT[:, 0, 0:2 * C], bT[:, 1, 0:2 * C], ALU.add).then_inc(s_init, 1)
                dve.tensor_copy(bsum[:, 2 * C:], bT[:, 0, 2 * C:]).then_inc(s_init, 1)
                dve.sem_inc(s_acc, 1)
                dve.wait_ge(s_gi_ev, 4 * MT)
                with dve.Fori(0, T // 2) as i:
                    for u in range(2):
                        t = i * 2
                        now = t + (u + 1)
                        h0, h1 = hT[:, u, :, :], hT[:, 1 - u, :, :]
                        def gi(g):
                            return gi2[:, bass.ds(i, 1), u, g, :, :].rearrange("p i c b -> p (i c) b")
                        dve.wait_ge(s_ps[R], now)
                        dve.transpose(trn[:, R, :], ps[R][:, 0:P]).then_inc(s_tr[R], 1)
                        dve.wait_ge(s_tr[R], now)
                        dve.tensor_tensor(pre[:, R], tr[R], gi(R), ALU.add).then_inc(s_pre[R], 1)
                        dve.wait_ge(s_ps[N], now)
                        dve.transpose(trn[:, N, :], ps[N][:, 0:P]).then_inc(s_tr[N], 1)
                        dve.wait_ge(s_tr[N], t + (u + 2))
                        dve.wait_ge(s_act[R], now)
                        dve.tensor_tensor(tmp[:, 0], tr[N], act[:, R], ALU.mult).then_inc(s_chain, 1)
                        dve.wait_ge(s_chain, t * 3 + (3 * u + 1))
                        dve.wait_ge(s_rb, t * 2 + (2 * u + 2))
                        dve.tensor_tensor(pre[:, N], tmp[:, 0], rbias[:, u, 1], ALU.add).then_inc(s_pre[N], 1)
                        dve.wait_ge(s_ps[Z], now)
                        dve.transpose(trn[:, Z, :], ps[Z][:, 0:P]).then_inc(s_tr[Z], 1)
                        dve.wait_ge(s_act[N], now)
                        dve.tensor_tensor(tmp[:, 1], h0, act[:, N], ALU.subtract).then_inc(s_chain, 1)
                        dve.wait_ge(s_chain, t * 3 + (3 * u + 2))
                        dve.wait_ge(s_act[Z], now)
                        dve.tensor_tensor(tmp[:, 2], tmp[:, 1], act[:, Z], ALU.mult).then_inc(s_chain, 1)
                        dve.wait_ge(s_chain, t * 3 + (3 * u + 3))
                        dve.wait_ge(s_acc, t + (u + 1))
                        dve.tensor_tensor(h1, tmp[:, 2], act[:, N], ALU.add).then_inc(s_h, 1)

            @block.scalar
            def _(a):
                a.wait_ge(s_init, 6)
                for blk in range(4):
                    for m in range(MT):
                        n = blk * MT + m
                        a.wait_ge(s_gi_mm, n + 1)
                        a.activation(gi4[:, TB * blk:TB * (blk + 1), m // C, m % C, :],
                                     pg[n % 4][:, :].rearrange("p (t b) -> p t b", b=B),
                                     ACT.Identity, bias=bsum[:, m:m + 1]).then_inc(s_gi_ev, 1)
                a.wait_ge(s_gi_ev, 4 * MT)
                for u in range(2):
                    a.copy(giz[:, u], gi4[:, u, Z]).then_inc(s_giz, 1)
                with a.Fori(0, T // 2) as i:
                    for u in range(2):
                        now = i * 2 + (u + 1)
                        for g, f in ((R, ACT.Sigmoid), (N, ACT.Tanh)):
                            a.wait_ge(s_pre[g], now)
                            a.activation(act[:, g], pre[:, g], f).then_inc(s_act[g], 1)
                        a.wait_ge(s_tr[Z], i * 2 + (u + 2))
                        a.activation(act[:, Z], tr[Z], ACT.Sigmoid).then_inc(s_act[Z], 1)
                        a.copy(giz[:, u], gi2[:, bass.ds(i + 1, 1), u, Z, :, :].rearrange("p i c b -> p (i c) b")).then_inc(s_giz, 1)

            @block.tensor
            def _(pe):
                pe.wait_ge(s_ld, NLD)
                for blk in range(4):
                    for m in range(MT):
                        n = blk * MT + m
                        if n >= 4:
                            pe.wait_ge(s_gi_ev, n - 3)
                        for k in range(C):
                            last = pe.matmul(pg[n % 4][:, :], wih[:, k, m * P:(m + 1) * P],
                                             xT[:, k, TB * blk:TB * (blk + 1), :].rearrange("p t b -> p (t b)"), start=k == 0, stop=k == C - 1)
                        last.then_inc(s_gi_mm, 1)
                pe.wait_ge(s_init, 4)
                with pe.Fori(0, T // 2) as i:
                    for u in range(2):
                        t = i * 2
                        pe.wait_ge(s_tr[N], t + (u + 1))
                        pe.wait_ge(s_tr[Z], t + (u + 1))
                        pe.wait_ge(s_giz, t + (u + 1))
                        for c in range(C):
                            for j in range(4):
                                pe.matmul(ps[Z][32 * j:32 * j + B, 32 * c:32 * c + 32], giz[:, u, c, :], identz[:, 32 * j:32 * j + 32], start=c == 0, stop=False)
                        if u == 1:
                            pe.wait_ge(s_h, t + 1)
                        else:
                            pe.wait_ge(s_acc, t + 1)
                        for g in (R, N, Z):
                            for c in range(C):
                                for j in range(4):
                                    o = g * D + P * j
                                    last = pe.matmul(ps[g][32 * j:32 * j + B, 0:P], hT[:, u, c, :], whh[:, c, o:o + P],
                                                     start=c == 0 and g != Z, stop=c == C - 1)
                            last.then_inc(s_ps[g], 1)
        gru.close()
        wkT = sb("wkT", [P, C, D]); woT = sb("woT", [P, C, D])
        ident = sb("identg", [P, P]); ones = sb("onesg", [P, P])
        rw = sb("rw", [64, 2, D])
        colv = sb("colv", [P, 2, C])
        br = sb("br", [P, C, NB, B])
        keys = sb("keys", [64, D]); kq = sb("kq", [64, D])
        st = sb("stt", [64, 8])
        row = sb("row", [1, 8, 64])
        attb = sb("attb", [P, NB * B])
        prod = sb("prod", [P, C, NB, B]); att = sb("att", [P, C, B]); pj = sb("pj", [P, C, B])
        eps = sb("eps", [P, 1])
        W5 = 512
        xa = sb("xa", [P, 2, C, W5]); sq = sb("sq", [P, 2, C, W5]); rs = sb("rs", [P, 2, W5])
        f_ld, f_v, f_pe, f_a, f_p = (sem(n) for n in ("last_loaded", "vector_steps", "tensor_steps", "scalar_steps", "normed_added"))
        f_x, f_mu, f_c, f_sq, f_var, f_sd, f_rs, f_n, f_gb = (sem(n) for n in (
            "shifted", "mean_ready", "centred", "squared", "variance_ready", "deviation_ready", "inverse_ready", "scaled", "gained"))
        f_o2 = [sem(f"written{i}") for i in range(2)]
        KP, BP, MU, VA = ps[0], ps[1], pg[0:2], pg[2:4]
        with nc.Block() as block:
            @block.sync
            def _(sp):
                sp.dma_start(wkT[:], wk).then_inc(f_ld, 16)
                sp.dma_start(woT[:], wo).then_inc(f_ld, 16)
                sp.dma_start(ident[:], ident_in).then_inc(f_ld, 16)
                for i in range(2):
                    sp.dma_start(rw[:, i, :], rowc[i:i + 1, :].to_broadcast([64, D])).then_inc(f_ld, 16)
                sp.dma_start(colv[:], cols).then_inc(f_ld, 16)
                for blk in range(4):
                    sp.wait_ge(f_p, blk + 1)
                    sp.dma_start(out[:, :, TB * blk:TB * (blk + 1), :].rearrange("p c t b -> p c (t b)"), sq[:, blk % 2]).then_inc(f_o2[blk % 2], 16)
                for q in f_o2:
                    sp.wait_ge(q, 32)

            @block.vector
            def _(dve):
                k = [0]
                def link(ins):
                    k[0] += 1
                    ins.then_inc(f_v, 1)
                    dve.wait_ge(f_v, k[0])
                dve.memset(eps[:], RMS_EPS)
                dve.memset(ones[:], 1.0).then_inc(f_v, 1)
                k[0] = 1
                for c in range(C):
                    dve.tensor_reduce(br[:, c], xT[:, c, :, :].rearrange("p (n i) b -> p n b i", n=NB), AX.X, ALU.add).then_inc(f_v, 1)
                k[0] += C
                dve.wait_ge(f_pe, 1)
                link(dve.tensor_copy(keys[:], KP[0:64, :]))
                dve.wait_ge(f_ld, 96)
                link(dve.tensor_tensor(kq[:], keys[:], keys[:], ALU.mult))
                link(dve.reduce_sum(st[:, 0:1], kq[:], AX.X))
                link(dve.tensor_scalar(st[:, 1:2], st[:, 0:1], 1.0 / D, RMS_EPS, ALU.mult, ALU.add))
                dve.wait_ge(f_a, 1)
                link(dve.reciprocal(st[:, 3:4], st[:, 2:3]))
                link(dve.tensor_scalar(kq[:], keys[:], st[:, 3:4], None, ALU.mult))
                link(dve.tensor_tensor(keys[:], kq[:], rw[:, 0, :], ALU.mult))
                link(dve.tensor_tensor(kq[:], keys[:], rw[:, 1, :], ALU.mult))
                link(dve.reduce_sum(st[:, 4:5], kq[:], AX.X))
                V_SCORE = k[0]
                dve.wait_ge(f_pe, 2)
                r = [row[0:1, i, :].rearrange("p (n b) -> p n b", b=B) for i in range(8)]
                link(dve.tensor_copy(row[0:1, 0, :], BP[0:1, 0:64]))
                link(dve.reduce_max(row[0:1, 1, 0:B], r[0].rearrange("p n b -> p b n"), AX.X))
                bc = lambda i: row[0:1, i, 0:B].rearrange("p (a b) -> p a b", a=1).to_broadcast([1, NB, B])
                link(dve.tensor_tensor(r[2], r[0], bc(1), ALU.subtract))
                dve.wait_ge(f_a, 2)
                link(dve.reduce_sum(row[0:1, 4, 0:B], r[3].rearrange("p n b -> p b n"), AX.X))
                link(dve.reciprocal(row[0:1, 5, 0:B], row[0:1, 4, 0:B]))
                link(dve.tensor_tensor(r[6], r[3], bc(5), ALU.mult))
                dve.wait_ge(f_pe, 3)
                link(dve.tensor_copy(attb[:], KP[:, 0:64]))
                for c in range(C):
                    dve.tensor_tensor(prod[:, c], br[:, c], attb[:].rearrange("p (n b) -> p n b", b=B), ALU.mult).then_inc(f_v, 1)
                k[0] += C
                dve.wait_ge(f_v, k[0])
                for c in range(C):
                    dve.tensor_reduce(att[:, c], prod[:, c].rearrange("p n b -> p b n"), AX.X, ALU.add).then_inc(f_v, 1)
                k[0] += C
                assert (V_SCORE, k[0]) == (14, 29), (V_SCORE, k[0])
                dve.wait_ge(f_pe, 4)
                link(dve.tensor_copy(pj[:], BP[:, 0:C * B].rearrange("p (c b) -> p c b", c=C)))

                def centre(blk):
                    h = blk % 2
                    dve.wait_ge(f_mu, blk + 1)
                    for c in range(C):
                        dve.scalar_tensor_tensor(xa[:, h, c], MU[h][:, :], -1.0 / D, xa[:, h, c], ALU.mult, ALU.add).then_inc(f_c, 1)

                def shift(blk):
                    h = blk % 2
                    if blk >= 2:
                        dve.wait_ge(f_gb, 4 * (blk - 1))
                    for c in range(C):
                        dve.tensor_tensor(xa[:, h, c].rearrange("p (t b) -> p t b", b=B), xT[:, c, TB * blk:TB * (blk + 1), :],
                                          pj[:, c:c + 1, :].to_broadcast([P, TB, B]), ALU.add).then_inc(f_x, 1)

                def scale(blk):
                    h = blk % 2
                    dve.wait_ge(f_sd, blk + 1)
                    dve.reciprocal(rs[:, h], rs[:, h]).then_inc(f_rs, 1)
                    dve.wait_ge(f_rs, blk + 1)
                    dve.wait_ge(f_c, 4 * blk + 4)
                    for c in range(C):
                        dve.tensor_tensor(xa[:, h, c], xa[:, h, c], rs[:, h], ALU.mult).then_inc(f_n, 1)
                shift(0)
                for blk in range(4):
                    centre(blk)
                    if blk + 1 < 4:
                        shift(blk + 1)
                    scale(blk)

            @block.tensor
            def _(pe):
                pe.wait_ge(f_ld, 96)
                pe.wait_ge(f_v, 1 + C)
                for c in range(C):
                    last = pe.matmul(KP[0:64, :], br[:, c].rearrange("p n b -> p (n b)"), wkT[:, c, :], start=c == 0, stop=c == C - 1)
                last.then_inc(f_pe, 1)
                pe.wait_ge(f_v, 14)
                pe.matmul(BP[0:1, 0:64], st[:, 4:5], ident[0:64, 0:64], start=True, stop=True).then_inc(f_pe, 1)
                pe.wait_ge(f_v, 20)
                pe.matmul(KP[:, 0:64], ones[0:1, :], row[0:1, 6, :], start=True, stop=True).then_inc(f_pe, 1)
                pe.wait_ge(f_v, 29)
                for m in range(C):
                    for c in range(C):
                        last = pe.matmul(BP[:, m * B:(m + 1) * B], woT[:, c, m * P:(m + 1) * P], att[:, c, :], start=c == 0, stop=c == C - 1)
                last.then_inc(f_pe, 1)

                def mean(blk):
                    h = blk % 2
                    pe.wait_ge(f_x, 4 * blk + 4)
                    if blk >= 2:
                        pe.wait_ge(f_c, 4 * (blk - 1))
                    for c in range(C):
                        last = pe.matmul(MU[h][:, :], ones[:], xa[:, h, c], start=c == 0, stop=c == C - 1)
                    last.then_inc(f_mu, 1)

                def var(blk):
                    h = blk % 2
                    pe.wait_ge(f_sq, 4 * blk + 4)
                    if blk >= 2:
                        pe.wait_ge(f_sd, blk - 1)
                    for c in range(C):
                        last = pe.matmul(VA[h][:, :], ones[:], sq[:, h, c], start=c == 0, stop=c == C - 1)
                    last.then_inc(f_var, 1)
                for blk in range(4):
                    mean(blk)
                    var(blk)

            @block.scalar
            def _(a):
                a.wait_ge(f_v, 9)
                a.activation(st[:, 2:3], st[:, 1:2], ACT.Sqrt).then_inc(f_a, 1)
                a.wait_ge(f_v, 17)
                a.activation(row[0:1, 3, :], row[0:1, 2, :], ACT.Exp).then_inc(f_a, 1)
                for blk in range(4):
                    h = blk % 2
                    for c in range(C):
                        a.wait_ge(f_c, 4 * blk + c + 1)
                        if blk >= 2:
                            a.wait_ge(f_o2[h], 16 * (blk // 2))
                        a.activation(sq[:, h, c], xa[:, h, c], ACT.Square).then_inc(f_sq, 1)
                    a.wait_ge(f_var, blk + 1)
                    if blk >= 2:
                        a.wait_ge(f_n, 4 * (blk - 1))
                    a.activation(rs[:, h], VA[h][:, :], ACT.Sqrt, scale=1.0 / D, bias=eps[:, 0:1]).then_inc(f_sd, 1)
                    for c in range(C):
                        a.wait_ge(f_n, 4 * blk + c + 1)
                        a.activation(sq[:, h, c], xa[:, h, c], ACT.Identity, scale=colv[:, 0, c:c + 1], bias=colv[:, 1, c:c + 1]).then_inc(f_gb, 1)

            @block.gpsimd
            def _(pool):
                for blk in range(4):
                    h = blk % 2
                    pool.wait_ge(f_gb, 4 * blk + 4)
                    pool.tensor_tensor(sq[:, h], sq[:, h], xT[:, :, TB * blk:TB * (blk + 1), :].rearrange("p c t b -> p c (t b)"), ALU.add).then_inc(f_p, 1)


def gru_inputs(v, np):
    f = lambda w: w.reshape(4, 4, 32, -1).transpose(0, 2, 1, 3).reshape(128, 4, -1)
    cp = lambda w: w.reshape(w.shape[0], -1, 4, 4, 32).transpose(0, 1, 3, 2, 4).reshape(w.shape)
    bt = lambda b: b.reshape(3, 4, 4, 32).transpose(1, 3, 0, 2).reshape(128, 12)
    col = lambda b: b.reshape(4, 4, 32).transpose(0, 2, 1).reshape(128, 4)
    return dict(cond=f(v['cond_2048'].T), w_ih=f(cp(v['L2_cond_W_ih'])), w_hh=f(v['L2_cond_W_hh']),
                b_ih=bt(v['L2_cond_b_ih']), b_hh=bt(v['L2_cond_b_hh']),
                wk=f(v['L3_cond_Wk'].T), wo=f(cp(v['L3_cond_Wo'].T)),
                rowc=np.stack([v['L3_cond_rms_weight'], v['cond_2048'][1]]),
                cols=np.stack([col(v['L3_cond_ln_gamma']), col(v['L3_cond_ln_beta'])], axis=1), ident=np.eye(128, dtype=np.float32))



ATTENTION = ("x", "mask", "wq0", "wk0", "wv0", "b0", "wq1", "wo1", "ident")
RECURRENT = ("cond", "w_ih", "w_hh", "b_ih", "b_hh", "wk", "wo", "rowc", "cols", "ident")


def build(nc, d, out):
    B, T, D = 8, 256, 512
    with nc.sbuf_tensor("xT", [128, D // 128, T, B], mybir.dt.float32) as xT:
        attention_layers(nc, xT, *(d[n] for n in ATTENTION))
        recurrent_and_last_layer(nc, xT, *(d[n] for n in RECURRENT), out)


def kernel(**inputs):
    import numpy as _np
    import concourse.bacc as _bacc
    from concourse import mybir as _mybir
    from concourse.bass_utils import run_bass_kernel_spmd as _run

    nc = _bacc.Bacc("TRN2", target_bir_lowering=False, num_devices=1)
    v = {k: _np.asarray(a) for k, a in inputs.items()}
    wt = lambda a: a.T.reshape(2, 128, 256).transpose(1, 0, 2)
    perm = lambda a: a.reshape(a.shape[:-1] + (4, 4, 32)).swapaxes(-3, -2).reshape(a.shape)
    ins = dict(x=perm(v['x']).reshape(8, 2, 128, 512).transpose(2, 1, 0, 3), mask=perm(v['cond_2048']),
               wq0=wt(v['L0_cond_Wq']), wk0=wt(v['L0_cond_Wk']), wv0=wt(v['L0_cond_Wv']), b0=v['L0_cond_b'],
               wq1=wt(v['L1_cond_Wq']), wo1=wt(v['L1_cond_Wo']), **gru_inputs(v, _np))
    arrays, d = {}, {}
    for name, a in ins.items():
        a = _np.ascontiguousarray(a)
        arrays[f"in_{name}_dram"] = a
        d[name] = nc.dram_tensor(f"in_{name}_dram", a.shape, _mybir.dt.from_np(a.dtype), kind="ExternalInput").ap()
    out = nc.dram_tensor("out_0_dram", (128, 4, 256, 8), _mybir.dt.float32, kind="ExternalOutput").ap()
    build(nc, d, out)
    r = _run(nc, [arrays], core_ids=[0])
    y = r.results[0]["out_0_dram"]
    return y.reshape(4, 32, 4, 256, 8).transpose(4, 3, 0, 2, 1).reshape(8, 256, 512)
```
